# Optimizing a Trainium2 kernel written in Bass

```python
import numpy as np
import jax
import jax.numpy as jnp

def _softmax(x, axis=-1):
    return jax.nn.softmax(x, axis=axis)

def _gelu(x):
    return jax.nn.gelu(x, approximate=True)

def _silu(x):
    return jax.nn.silu(x)

def _sigmoid(x):
    return jax.nn.sigmoid(x)

def _layernorm(x, axis=-1, eps=1e-05):
    m = jnp.mean(x, axis=axis, keepdims=True)
    v = jnp.var(x, axis=axis, keepdims=True)
    return (x - m) / jnp.sqrt(v + eps)

def _scatter_add(tgt, idx, src, axis=0):
    return tgt.at[idx].add(src)

def _segment_sum(src, seg, n):
    return jax.ops.segment_sum(src, seg, n)
kernel_name = 'mk_macaron_d1_jaxref_r4_c7fbf4'

def setup_inputs(seed: int=0):
    np.random.seed(seed)
    _w = jnp.asarray

    def _L0_attn_setup():
        import jax, jax.numpy as jnp
        import numpy as np
        B, S, D, G = (2, 512, 256, 8)
        key = jax.random.key(seed)
        ks = jax.random.split(key, 7)
        w = 0.02
        return {'hidden_states': jax.random.normal(ks[0], (B, S, D), jnp.float32), 'Wq': jax.random.normal(ks[1], (D, D), jnp.float32) * w, 'bq': jax.random.normal(ks[2], (D,), jnp.float32) * w, 'Wk': jax.random.normal(ks[3], (D, D), jnp.float32) * w, 'bk': jax.random.normal(ks[4], (D,), jnp.float32) * w, 'Wv': jax.random.normal(ks[5], (D, D), jnp.float32) * w, 'bv': jax.random.normal(ks[6], (D,), jnp.float32) * w}
    _L0_attn_in = _L0_attn_setup()

    def _L0_ffn_setup():
        import jax, jax.numpy as jnp
        import numpy as np
        D = 256
        H = 16
        HD = D // H
        L = 64
        E = 8
        B, T = (4, 512)
        EPS = 1e-06

        def _glorot(k, shape):
            fan_in, fan_out = (shape[-2], shape[-1])
            lim = np.sqrt(6.0 / (fan_in + fan_out)).astype(np.float32)
            return jax.random.uniform(k, shape, jnp.float32, -lim, lim)

        def _rmsnorm(x, gamma):
            return gamma * x * jax.lax.rsqrt(jnp.mean(x * x, axis=-1, keepdims=True) + EPS)
        key = jax.random.key(seed)
        ks = jax.random.split(key, 8)
        return {'x': jax.random.normal(ks[0], (B, T, D), jnp.float32), 'gamma1': jnp.ones((D,), jnp.float32), 'Wq': _glorot(ks[1], (D, D)), 'bq': jnp.zeros((D,), jnp.float32), 'Wdown': _glorot(ks[2], (D, L)), 'bdown': jnp.zeros((L,), jnp.float32), 'Wup': _glorot(ks[3], (L, 2 * D)), 'bup': jnp.zeros((2 * D,), jnp.float32), 'Wo': _glorot(ks[4], (D, D)), 'bo': jnp.zeros((D,), jnp.float32), 'gamma2': jnp.ones((D,), jnp.float32), 'Wg': _glorot(ks[5], (D, E)), 'bg': jnp.zeros((E,), jnp.float32), 'We': _glorot(ks[6], (E, D, D))}
    _L0_ffn_in = _L0_ffn_setup()
    _d = {'L0_attn_hidden_states': _L0_attn_in['hidden_states'], 'L0_attn_Wq': _L0_attn_in['Wq'], 'L0_attn_bq': _L0_attn_in['bq'], 'L0_attn_Wk': _L0_attn_in['Wk'], 'L0_attn_bk': _L0_attn_in['bk'], 'L0_attn_Wv': _L0_attn_in['Wv'], 'L0_attn_bv': _L0_attn_in['bv'], 'L0_ffn_gamma1': _L0_ffn_in['gamma1'], 'L0_ffn_Wq': _L0_ffn_in['Wq'], 'L0_ffn_bq': _L0_ffn_in['bq'], 'L0_ffn_Wdown': _L0_ffn_in['Wdown'], 'L0_ffn_bdown': _L0_ffn_in['bdown'], 'L0_ffn_Wup': _L0_ffn_in['Wup'], 'L0_ffn_bup': _L0_ffn_in['bup'], 'L0_ffn_Wo': _L0_ffn_in['Wo'], 'L0_ffn_bo': _L0_ffn_in['bo'], 'L0_ffn_gamma2': _L0_ffn_in['gamma2'], 'L0_ffn_Wg': _L0_ffn_in['Wg'], 'L0_ffn_bg': _L0_ffn_in['bg'], 'L0_ffn_We': _L0_ffn_in['We']}
    _x0 = _d['L0_attn_hidden_states']
    _d['L0_attn_hidden_states'] = jax.random.normal(jax.random.fold_in(jax.random.key(seed), 1), (8, 512, 256), dtype=_x0.dtype)
    del _x0
    return _d

def reference(L0_attn_hidden_states, L0_attn_Wq, L0_attn_bq, L0_attn_Wk, L0_attn_bk, L0_attn_Wv, L0_attn_bv, L0_ffn_gamma1, L0_ffn_Wq, L0_ffn_bq, L0_ffn_Wdown, L0_ffn_bdown, L0_ffn_Wup, L0_ffn_bup, L0_ffn_Wo, L0_ffn_bo, L0_ffn_gamma2, L0_ffn_Wg, L0_ffn_bg, L0_ffn_We):

    def _L0_attn_ref(hidden_states, Wq, bq, Wk, bk, Wv, bv):
        import jax, jax.numpy as jnp
        import numpy as np
        B, S, D, G = (2, 512, 256, 8)
        b, n, d = hidden_states.shape
        g = G
        h = d // g
        scale = jnp.sqrt(jnp.asarray(d, jnp.float32))
        q = (hidden_states @ Wq + bq).reshape(b, n, g, h)
        k = (hidden_states @ Wk + bk).reshape(b, n, g, h)
        v = (hidden_states @ Wv + bv).reshape(b, n, g, h)
        scores = jnp.einsum('bngh,bmgh->bnmg', q, k) / scale
        probs = jax.nn.softmax(scores, axis=-1)
        ctx = jnp.einsum('bnmg,bmgh->bngh', probs, v).reshape(b, n, d)
        return ctx

    def _L0_ffn_ref(x, gamma1, Wq, bq, Wdown, bdown, Wup, bup, Wo, bo, gamma2, Wg, bg, We):
        import jax, jax.numpy as jnp
        import numpy as np
        D = 256
        H = 16
        HD = D // H
        L = 64
        E = 8
        B, T = (4, 512)
        EPS = 1e-06

        def _glorot(k, shape):
            fan_in, fan_out = (shape[-2], shape[-1])
            lim = np.sqrt(6.0 / (fan_in + fan_out)).astype(np.float32)
            return jax.random.uniform(k, shape, jnp.float32, -lim, lim)

        def _rmsnorm(x, gamma):
            return gamma * x * jax.lax.rsqrt(jnp.mean(x * x, axis=-1, keepdims=True) + EPS)
        b, t = (x.shape[0], x.shape[1])
        h = _rmsnorm(x, gamma1)
        q = (h @ Wq + bq).reshape(b, t, H, HD)
        kv = ((h @ Wdown + bdown) @ Wup + bup).reshape(b, t, H, 2 * HD)
        k, v = jnp.split(kv, 2, axis=-1)
        att = jnp.einsum('bthd,btgd->bthg', q, k) / np.sqrt(HD).astype(np.float32)
        att = jax.nn.softmax(att, axis=-1)
        out = jnp.einsum('bthg,btgd->bthd', att, v).reshape(b, t, D)
        x = x + (out @ Wo + bo)
        h2 = _rmsnorm(x, gamma2)
        gate = jax.nn.softmax(h2 @ Wg + bg, axis=-1)
        combined = jnp.einsum('btd,edf,bte->btf', h2, We, gate)
        return x + combined
    x = L0_attn_hidden_states
    x = x + 0.5 * _L0_ffn_ref(_layernorm(x, axis=-1), L0_ffn_gamma1, L0_ffn_Wq, L0_ffn_bq, L0_ffn_Wdown, L0_ffn_bdown, L0_ffn_Wup, L0_ffn_bup, L0_ffn_Wo, L0_ffn_bo, L0_ffn_gamma2, L0_ffn_Wg, L0_ffn_bg, L0_ffn_We)
    x = x + _L0_attn_ref(_layernorm(x, axis=-1), L0_attn_Wq, L0_attn_bq, L0_attn_Wk, L0_attn_bk, L0_attn_Wv, L0_attn_bv)
    x = x + 0.5 * _L0_ffn_ref(_layernorm(x, axis=-1), L0_ffn_gamma1, L0_ffn_Wq, L0_ffn_bq, L0_ffn_Wdown, L0_ffn_bdown, L0_ffn_Wup, L0_ffn_bup, L0_ffn_Wo, L0_ffn_bo, L0_ffn_gamma2, L0_ffn_Wg, L0_ffn_bg, L0_ffn_We)
    return x

_drawn_inputs = setup_inputs


def setup_inputs(seed=0):
    import zlib

    import numpy as np

    out = dict(_drawn_inputs(seed))
    spreads = {'L0_ffn_gamma1': (1.0, 0.6),
     'L0_ffn_bq': (0.0, 0.8),
     'L0_ffn_bdown': (0.0, 0.293),
     'L0_ffn_bup': (0.0, 0.1),
     'L0_ffn_bo': (0.0, 0.1),
     'L0_ffn_gamma2': (1.0, 0.2),
     'L0_ffn_bg': (0.0, 0.767)}
    factors = {'L0_attn_bq': 33.769, 'L0_attn_bk': 33.661}
    for name, (base, spread) in spreads.items():
        noise = np.random.default_rng([zlib.crc32(name.encode()), seed]).standard_normal(out[name].shape)
        drawn = base * np.exp(spread * noise) if base else spread * noise
        out[name] = jnp.asarray(drawn.astype(out[name].dtype))
    for name, factor in factors.items():
        out[name] = (out[name] * factor).astype(out[name].dtype)
    return out
```

```python
from contextlib import ExitStack

import concourse.bass as bass
from concourse import mybir

F32 = mybir.dt.float32
F32R = mybir.dt.float32r
ALU = mybir.AluOpType
ACT = mybir.ActivationFunctionType
AX = mybir.AxisListType

P = 128
BANK = 512
LN_EPS = 1e-5
RMS_EPS = 1e-6


class Signal:

    def __init__(self, sem, step=1):
        self.sem, self.step, self.count = sem, step, 0

    def next(self):
        self.count += self.step
        return (self, self.count)


class Lane:

    def __init__(self):
        self.items = []

    def do(self, emit, after=(), done=None):
        value = done.next() if done is not None else None
        self.items.append((emit, tuple(after), value))
        return value

    def hold(self, sig, value):
        self.items.append((None, ((sig, value),), None))

    def issue(self, eng):
        passed = {}
        for emit, after, value in self.items:
            for sig, need in after:
                if passed.get(id(sig), 0) < need:
                    eng.wait_ge(sig.sem, need)
                    passed[id(sig)] = need
            if emit is None:
                continue
            ins = emit(eng)
            if value is not None:
                ins.then_inc(value[0].sem, value[0].step)
        self.items = []


def interleave(*lists):
    live = [[g, n, 0] for g, n in lists if g is not None]
    while live:
        live.sort(key=lambda x: x[2] / x[1])
        g = live[0]
        g[2] += 1
        try:
            next(g[0])
        except StopIteration:
            live.pop(0)


def macaron(nc, a, out):
    x_dram = a["L0_attn_hidden_states"]
    B, S, D = x_dram.shape
    NT = S // P
    KC = D // P
    L = a["L0_ffn_Wdown"].shape[1]
    E = a["L0_ffn_We"].shape[0]
    H, HD = 16, D // 16
    G = 8
    GD = D // G
    T8 = P // HD
    NR = 32
    CR = NR // 2
    HQ = P // GD
    NHG = G // HQ
    assert S == BANK and KC == 2 and 2 * L == P and T8 == 8 and HD == 16 and HQ == 4

    ctx = ExitStack()
    with ctx:
        def sem(name, step=1):
            return Signal(ctx.enter_context(nc.semaphore(name)), step)

        def sbt(scope, name, shape, dt=F32):
            return scope.enter_context(nc.sbuf_tensor(name, shape, dt))

        PE, DVE, SCA, POOL, SP = Lane(), Lane(), Lane(), Lane(), Lane()

        s_pe, s_dve, s_act, s_pool = sem("s_pe"), sem("s_dve"), sem("s_act"), sem("s_pool")
        s_x = [sem(f"s_x{b}", 16) for b in range(B)]
        s_w = [sem(f"s_w{n}", 16) for n in range(30)]
        s_out = sem("s_out", 16)

        def pe(emit, after=()):
            return PE.do(emit, after, s_pe)

        def dve(emit, after=()):
            return DVE.do(emit, after, s_dve)

        def act(emit, after=()):
            return SCA.do(emit, after, s_act)

        def pool(emit, after=()):
            return POOL.do(emit, after, s_pool)

        psum = ctx.enter_context(nc.psum_tensor("psum", [P, 8, BANK], F32))
        bank_read = [[] for _ in range(8)]

        X = sbt(ctx, "X", [P, B, NT, D])
        ident = sbt(ctx, "ident", [P, P])
        mask8 = sbt(ctx, "mask8", [P, T8])
        half_neg = sbt(ctx, "half_neg", [P, 8])
        row1 = sbt(ctx, "row1", [2, 1])
        ones2f = sbt(ctx, "ones2f", [2, P])
        ones2 = sbt(ctx, "ones2", [2, P], F32R)
        wq = sbt(ctx, "wq", [P, 2, KC, D], F32R)
        wo = sbt(ctx, "wo", [P, 2, KC, D], F32R)
        wd = sbt(ctx, "wd", [P, 2, KC, 2 * L], F32R)
        wu = sbt(ctx, "wu", [P, 2, 2 * D], F32R)
        wg = sbt(ctx, "wg", [P, 2, KC, E], F32R)
        NB = D + 2 * D + D + E + D
        BQ, BU, BO, BG, BV = 0, D, 3 * D, 4 * D, 4 * D + E
        bias = sbt(ctx, "bias", [2, NB], F32R)
        gam = sbt(ctx, "gam", [P, 2, KC])
        bdn = sbt(ctx, "bdn", [P, 1])
        abq = sbt(ctx, "abq", [P, 2, KC])

        with ExitStack() as scope:
            n_w = [0]

            def load(dst, src, columns=False):
                s = s_w[n_w[0]]
                n_w[0] += 1
                return SP.do(lambda e: e.dma_start(dst, src, allow_slow_non_contiguous=columns), (), s)

            for b in range(2):
                SP.do(lambda e, b=b: e.dma_start(X[:, b, :, :], x_dram[b].rearrange("(p i) d -> p i d", i=NT)), (), s_x[b])
            raw_q = sbt(scope, "raw_q", [P, KC, D])
            raw_o = sbt(scope, "raw_o", [P, KC, D])
            raw_d = sbt(scope, "raw_d", [P, KC, 2, L])
            raw_u = sbt(scope, "raw_u", [P, 2 * D])
            raw_g = sbt(scope, "raw_g", [P, KC, E])
            raw_b = sbt(scope, "raw_b", [2, NB])
            bhi = sbt(scope, "bhi", [2, NB], F32R)
            t_q = load(raw_q[:, :, :], a["L0_ffn_Wq"].rearrange("(k c) n -> c k n", c=P))
            t_d = [load(raw_d[:, :, r, :], a["L0_ffn_Wdown"].rearrange("(k c) n -> c k n", c=P)) for r in range(2)]
            t_u = [load(raw_u[r * L:(r + 1) * L, :], a["L0_ffn_Wup"]) for r in range(2)]
            t_b = []
            for at, name in ((BQ, "L0_ffn_bq"), (BU, "L0_ffn_bup"), (BO, "L0_ffn_bo"), (BG, "L0_ffn_bg"), (BV, "L0_attn_bv")):
                src = a[name]
                for r in range(2):
                    t_b.append(load(raw_b[r:r + 1, at:at + src.shape[0]], src.rearrange("(o n) -> o n", o=1)))
            t_gam = [load(gam[:, n, :], a[name].rearrange("(k c) -> c k", c=P), True)
                     for n, name in enumerate(("L0_ffn_gamma1", "L0_ffn_gamma2"))]
            t_abq = [load(abq[:, n, :], a[name].rearrange("(k c) -> c k", c=P), True)
                     for n, name in enumerate(("L0_attn_bq", "L0_attn_bk"))]
            t_bdn = [load(bdn[r * L:(r + 1) * L, :], a["L0_ffn_bdown"].rearrange("(n o) -> n o", o=1)) for r in range(2)]
            t_o = load(raw_o[:, :, :], a["L0_ffn_Wo"].rearrange("(k c) n -> c k n", c=P))
            t_g = load(raw_g[:, :, :], a["L0_ffn_Wg"].rearrange("(k c) n -> c k n", c=P))
            for b in range(2, B):
                SP.do(lambda e, b=b: e.dma_start(X[:, b, :, :], x_dram[b].rearrange("(p i) d -> p i d", i=NT)), (), s_x[b])

            SCA.do(lambda e: e.preload_act_table_set("natural_log_exp_and_others"))
            t = pool(lambda e: e.memset(ident[:, :], 0.0))
            t_id = pool(lambda e: e.affine_select(out=ident[:, :], in_=ident[:, :], compare_op=ALU.not_equal, fill=1.0,
                                                  base=0, pattern=[[-1, P]], channel_multiplier=1), [t])
            pool(lambda e: e.memset(half_neg[:, :], -0.5))
            t_1 = pool(lambda e: e.memset(ones2f[:, :], 1.0))
            dve(lambda e: e.tensor_reduce(mask8[:, :], ident[:, :].rearrange("p (t c) -> p t c", t=T8), AX.X, ALU.add), [t_id])
            t_r = dve(lambda e: e.tensor_copy(row1[:, :], ident[0:2, 1:2]), [t_id])
            dve(lambda e: e.tensor_copy(ones2[:, :], ones2f[:, :]), [t_1])

            def split(dst_hi, dst_lo, src, landed):
                th = act(lambda e: e.activation(dst_hi, src, ACT.Copy), landed)
                dve(lambda e: e.tensor_tensor(dst_lo, src, dst_hi.bitcast(F32), ALU.subtract), [th, *landed])

            split(wq[:, 0], wq[:, 1], raw_q[:, :, :], [t_q])
            split(wd[:, 0], wd[:, 1], raw_d[:, :, :, :].rearrange("p k r l -> p k (r l)"), t_d)
            split(wu[:, 0], wu[:, 1], raw_u[:, :], t_u)
            t = act(lambda e: e.activation(bhi[:, :], raw_b[:, :], ACT.Copy), t_b)
            t = dve(lambda e: e.tensor_scalar(bhi[:, :], bhi[:, :].bitcast(F32), row1[:, 0:1], None, ALU.mult), [t, t_r])
            dve(lambda e: e.tensor_tensor(bias[:, :], raw_b[:, :], bhi[:, :].bitcast(F32), ALU.subtract), [t])
            split(wo[:, 0], wo[:, 1], raw_o[:, :, :], [t_o])
            split(wg[:, 0], wg[:, 1], raw_g[:, :, :], [t_g])
            for sig, value in (*t_gam, *t_abq, *t_bdn):
                SP.hold(sig, value)
            with nc.Block() as block:
                _issue(block, PE, DVE, SCA, POOL, SP)

        def stats(row, mv, rs, raw, width_rms):
            for i in range(NT):
                t = dve(lambda e, i=i: e.bn_stats(raw[:, i, :], X[:, row, i, :]), x_ready[row])
            for i in range(NT):
                t = dve(lambda e, i=i: e.bn_aggr(mv[:, i, :], raw[:, i, :]), [t])
            var = mv[:, :, 1]
            t = pool(lambda e: e.tensor_scalar(rs[:, 3, :], var, LN_EPS, None, ALU.add), [t])
            t = pool(lambda e: e.tensor_tensor(rs[:, 0, :], rs[:, 3, :], half_neg[:, 0:NT], ALU.pow), [t])
            if width_rms:
                t = pool(lambda e: e.tensor_tensor(rs[:, 3, :], var, rs[:, 0, :], ALU.mult), [t])
                t = pool(lambda e: e.tensor_tensor(rs[:, 3, :], rs[:, 3, :], rs[:, 0, :], ALU.mult), [t])
                t = pool(lambda e: e.tensor_scalar(rs[:, 3, :], rs[:, 3, :], RMS_EPS, None, ALU.add), [t])
                t = pool(lambda e: e.tensor_tensor(rs[:, 1, :], rs[:, 3, :], half_neg[:, 0:NT], ALU.pow), [t])
                t = pool(lambda e: e.tensor_tensor(rs[:, 2, :], rs[:, 1, :], rs[:, 0, :], ALU.mult), [t])
            return t

        def transposed_split(src, hl, bank, k, gamma, ready, hl_free):
            for i in range(NT):
                t = pe(lambda e, i=i: e.transpose(psum[:, bank, i * P:(i + 1) * P], src[:, i, k * P:(k + 1) * P], ident[:, :]),
                       [*ready, *bank_read[bank]])
            hi, lo, ps = hl[:, 0, k, :], hl[:, 1, k, :], psum[:, bank, :]
            th = act(lambda e: e.activation(hi, ps, ACT.Copy, scale=gamma), [t, *hl_free])
            tl = dve(lambda e: e.scalar_tensor_tensor(out=lo, in0=ps, scalar=gamma, in1=hi.bitcast(F32),
                                                      op0=ALU.mult, op1=ALU.subtract), [th])
            bank_read[bank] = [tl]
            return [th, tl], t

        def product(out_ap, terms, after, bias_at=None, width=0):
            if bias_at is not None:
                terms = [*terms, (ones2[:, :], bias[:, bias_at:bias_at + width])]
            for n, (l, r) in enumerate(terms):
                t = pe(lambda e, l=l, r=r, n=n: e.matmul(out_ap, l, r, start=(n == 0), stop=(n == len(terms) - 1)),
                       after if n == 0 else ())
            return t

        def three(hl, i, w):
            cols = slice(i * P, (i + 1) * P)
            return [(hl[:, x, k, cols], w[:, y, k]) for k in range(KC) for x, y in ((0, 0), (1, 0), (0, 1))]

        x_ready = [[(s_x[b], 16)] for b in range(B)]

        def ffn(tag):
            with ExitStack() as scope:
                def sb(name, shape, dt=F32):
                    return sbt(scope, f"{name}{tag}", shape, dt)

                raw = sb("bn_raw", [P, NT, 6])
                mv = [sb(f"mv{n}", [P, NT, 2]) for n in range(3)]
                rs = [sb(f"rs{n}", [P, 4, NT]) for n in range(3)]
                xs = sb("xs", [P, NT, D])
                hT = sb("hT", [P, 2, KC, S], F32R)
                la = sb("la", [P, S], F32R)
                qc = [sb(f"qc{n}", [P, NR * H + H]) for n in range(3)]
                kvc = [sb(f"kvc{n}", [P, NR, 2, HD]) for n in range(3)]
                kvx = [sb(f"kvx{n}", [P, CR, 2, T8, HD]) for n in range(2)]
                ex = [sb(f"ex{n}", [P, BANK]) for n in range(2)]
                mx = [sb(f"mx{n}", [P, NR]) for n in range(2)]
                sm = [sb(f"sm{n}", [P, NR]) for n in range(2)]
                rc = [sb(f"rc{n}", [P, NR]) for n in range(3)]
                at = [sb(f"at{n}", [P, CR * H + H]) for n in range(2)]
                on = [sb(f"on{n}", [P, BANK]) for n in range(2)]
                ot = [sb(f"ot{n}", [P, 2, D]) for n in range(2)]
                oT = sb("oT", [P, 2, KC, S], F32R)
                x1 = sb("x1", [P, NT, D])
                xs2 = sb("xs2", [P, NT, D])
                ssq = [sb(f"ssq{n}", [P, NT]) for n in range(2)]
                rms = [sb(f"rms{n}", [P, NT]) for n in range(2)]
                h2 = [sb(f"h2{n}", [P, 2, KC, S], F32R) for n in range(2)]
                gl = sb("gl", [P, NT, E])
                gs = sb("gs", [P, 3, NT])
                gate = [sb(f"gate{n}", [P, NT, E]) for n in range(2)]
                y = sb("y", [P, 4, D])

                we = sb("we", [P, 2, KC, E, D], F32R)
                negm = [sb(f"negm{n}", [P, 2, NT]) for n in range(3)]
                s_we = [sem(f"s_we{tag}{k}", 16) for k in range(KC)]
                t_we = []
                for k in range(KC):
                    raw_e = kvx[1][:, k * CR // KC:(k + 1) * CR // KC].rearrange("p r w t d -> p (r w t d)").rearrange(
                        "p (e n) -> p e n", e=E)
                    t = SP.do(lambda e, k=k, raw_e=raw_e: e.dma_start(
                        raw_e, a["L0_ffn_We"][:, k * P:(k + 1) * P, :].rearrange("e c n -> c e n")), (), s_we[k])
                    th = act(lambda e, k=k, raw_e=raw_e: e.activation(we[:, 0, k], raw_e, ACT.Copy), [t])
                    t_we.append(dve(lambda e, k=k, raw_e=raw_e: e.tensor_tensor(
                        we[:, 1, k], raw_e, we[:, 0, k].bitcast(F32), ALU.subtract), [th]))
                for q in qc:
                    t_pad = pool(lambda e, q=q: e.memset(q[:, NR * H:], 0.0))
                for q in at:
                    t_pad = pool(lambda e, q=q: e.memset(q[:, CR * H:], 0.0))

                free = {("kvx", 1): t_we}
                ready = {}
                singles = [5, 6, 7]
                turn = [0, 0]

                def single():
                    turn[0] += 1
                    return singles[turn[0] % 3]

                def front(s):
                    m, r = mv[s % 3], rs[s % 3]
                    nm = negm[s % 3]
                    t = stats(s, m, r, raw, True)
                    for n, of in ((0, 2), (1, 0)):
                        t = pool(lambda e, n=n, of=of: e.tensor_tensor(nm[:, n, :], m[:, :, 0], r[:, of, :], ALU.mult), [t])
                        t = pool(lambda e, n=n: e.tensor_scalar(nm[:, n, :], nm[:, n, :], -1.0, 0.0, ALU.mult, ALU.add), [t])
                    ready["rs", s] = t
                    yield
                    for i in range(NT):
                        tx = pool(lambda e, i=i: e.tensor_scalar(xs[:, i, :], X[:, s, i, :], r[:, 2, i:i + 1], nm[:, 0, i:i + 1],
                                                                 ALU.mult, ALU.add), [t, *free.get("xs", [])])
                    yield
                    hs = []
                    for k in range(KC):
                        tt, tp = transposed_split(xs, hT, single(), k, gam[:, 0, k:k + 1], [tx], free.get("hT", []))
                        hs += tt
                        free["xs"] = [tp]
                        yield
                    b = single()
                    terms = [(wd[:, y_, k, :], hT[:, x_, k, :]) for k in range(KC) for x_, y_ in ((0, 0), (1, 0), (0, 1))]
                    t = product(psum[:, b, :], terms, [*hs, *bank_read[b]])
                    tm = act(lambda e: e.activation(la[:, :], psum[:, b, :], ACT.Identity, bias=bdn[:, 0:1]), [t, *free.get("la", [])])
                    up = slice(L, 2 * L)
                    tl = dve(lambda e: e.scalar_tensor_tensor(out=la[up, :], in0=psum[up, b, :], scalar=bdn[up, 0:1],
                                                              in1=la[up, :].bitcast(F32), op0=ALU.add, op1=ALU.subtract), [tm])
                    bank_read[b] = [tl]
                    yield
                    for p in range(NT // 2):
                        n = (2 * s + p) % 3
                        bq = single()
                        for i in (2 * p, 2 * p + 1):
                            t = product(psum[:, bq, (i % 2) * D:(i % 2 + 1) * D], three(hT, i, wq), [*hs, *bank_read[bq]], BQ, D)
                        src = psum[:, bq, :].rearrange("p (b h d) -> p h b d", b=2, h=H)
                        dst = qc[n][:, 0:NR * H].rearrange("p (r h) -> p h r", h=H)
                        tq = dve(lambda e, src=src, dst=dst: e.transpose(dst, src), [t, *free.get(("qc", n), [])])
                        bank_read[bq] = [tq]
                        yield
                        for i in (2 * p, 2 * p + 1):
                            terms = [(la[:, i * P:(i + 1) * P], wu[:, y_, :]) for y_ in (0, 1)]
                            bk = 3 + i % 2
                            t = product(psum[:, bk, :], terms, [tl, *bank_read[3], *bank_read[4]], BU, 2 * D)
                        kv = psum[:, 3:5, :].rearrange("p b (g w d) -> p w b g d", w=2, d=HD)
                        src_k = kv[:, 0].rearrange("p b g d -> p g b d")
                        src_v = kv[:, 1].rearrange("p b g d -> p d b g")
                        fr = [t, *free.get(("kvc", n), [])]
                        dst = kvc[n][:, :, 0, :].rearrange("p r h -> p h r")
                        dve(lambda e, s_=src_k, dst=dst: e.transpose(dst, s_), fr)
                        dst = kvc[n][:, :, 1, :].rearrange("p r h -> p h r")
                        tk = dve(lambda e, s_=src_v, dst=dst: e.transpose(dst, s_), fr)
                        bank_read[3] = bank_read[4] = [tk]
                        ready["qkv", 2 * s + p] = [tq, tk]
                        yield
                    free["hT"] = free["la"] = [t]

                def expand(c):
                    pr, half = c // 2, c % 2
                    src = kvc[pr % 3][:, half * CR:(half + 1) * CR, :, :].rearrange("p r w d -> p (r w) d")
                    dst = kvx[c % 2][:, :, :, :, :].rearrange("p r w t d -> p (r w) t d")
                    fr = [*ready["qkv", pr], *free.get(("kvx", c % 2), [])]
                    toks = {}
                    for t8 in range(T8):
                        o, m = dst[:, :, t8, :], mask8[:, t8:t8 + 1]
                        who = EXPAND[t8]
                        if who == "V":
                            toks[who] = dve(lambda e, o=o, m=m: e.tensor_scalar(o, src, m, None, ALU.mult), fr)
                        elif who == "A":
                            toks[who] = act(lambda e, o=o, m=m: e.activation(o, src, ACT.Copy, scale=m), fr)
                        else:
                            toks[who] = pool(lambda e, o=o, m=m: e.tensor_scalar(o, src, m, 1.0, ALU.mult, ALU.mult), fr)
                    free["kvc", pr % 3] = [*free.get(("kvc", pr % 3), []), *toks.values()] if half else list(toks.values())
                    ready["kvx", c] = list(toks.values())

                def scores(c):
                    pr, half = c // 2, c % 2
                    b = single()
                    q, kx = qc[pr % 3], kvx[c % 2]
                    for r in range(CR):
                        j, a4 = r % 4, r // 4
                        at0 = (half * CR + r) * H
                        t = pe(lambda e, r=r, j=j, a4=a4, at0=at0: e.matmul(
                            psum[32 * j:32 * j + 32, b, a4 * P:(a4 + 1) * P], q[:, at0:at0 + 32], kx[:, r, 0, :, :],
                            start=True, stop=True), [*ready["kvx", c], *bank_read[b], t_pad])
                    free["qc", pr % 3] = [t]
                    e_, m_, s_, r_ = ex[c % 2], mx[c % 2], sm[c % 2], rc[c % 3]
                    ps = psum[:, b, :].rearrange("p (t g) -> p t g", g=H)
                    ev = e_[:, :].rearrange("p (t g) -> p t g", g=H)
                    t = dve(lambda e: e.tensor_reduce(m_[:, :], ps, AX.X, ALU.max), [t])
                    t = dve(lambda e: e.tensor_tensor(ev, ps, m_[:, :].unsqueeze(2).to_broadcast([P, NR, H]), ALU.subtract),
                            [t, *free.get(("ex", c % 2), [])])
                    bank_read[b] = [t]
                    t = act(lambda e: e.activation(e_[:, :], e_[:, :], ACT.Exp, scale=float(HD) ** -0.5), [t])
                    ready["ex", c] = [t]
                    t = dve(lambda e: e.tensor_reduce(s_[:, :], ev, AX.X, ALU.add), [t])
                    t = dve(lambda e: e.reciprocal(r_[:, :], s_[:, :]), [t])
                    ready["rc", c] = [t]

                def turn_probs(c):
                    b = single()
                    for a4 in range(4):
                        t = pe(lambda e, a4=a4: e.transpose(psum[:, b, a4 * P:(a4 + 1) * P], ex[c % 2][:, a4 * P:(a4 + 1) * P],
                                                            ident[:, :]), [*ready["ex", c], *bank_read[b]])
                    free["ex", c % 2] = [t]
                    src = psum[:, b, :].rearrange("p (r h) -> p r h", h=32)[:, :, 0:H]
                    dst = at[c % 2][:, 0:CR * H].rearrange("p (r h) -> p r h", h=H)
                    t = act(lambda e: e.activation(dst, src, ACT.Copy), [t, *free.get(("at", c % 2), [])])
                    bank_read[b] = [t]
                    ready["at", c] = [t]

                def attend(c):
                    b = single()
                    for r in range(CR):
                        j, a4 = r % 4, r // 4
                        t = pe(lambda e, r=r, j=j, a4=a4: e.matmul(
                            psum[32 * j:32 * j + 32, b, a4 * P:(a4 + 1) * P], at[c % 2][:, r * H:r * H + 32],
                            kvx[c % 2][:, r, 1, :, :], start=True, stop=True), [*ready["at", c], *bank_read[b], t_pad])
                    free["at", c % 2] = free["kvx", c % 2] = [t]
                    ps = psum[:, b, :].rearrange("p (t d) -> p t d", d=HD)
                    ov = on[c % 2][:, :].rearrange("p (t d) -> p t d", d=HD)
                    t = dve(lambda e: e.tensor_tensor(ov, ps, rc[c % 3][:, :].unsqueeze(2).to_broadcast([P, NR, HD]), ALU.mult),
                            [t, *ready["rc", c], *free.get(("on", c % 2), [])])
                    bank_read[b] = [t]
                    ready["on", c] = [t]

                def turn_out(pr):
                    for half in range(2):
                        for a4 in range(4):
                            t = pe(lambda e, a4=a4, half=half: e.transpose(
                                psum[:, 3 + half, a4 * P:(a4 + 1) * P], on[half][:, a4 * P:(a4 + 1) * P], ident[:, :]),
                                [*ready["on", 2 * pr + half], *bank_read[3], *bank_read[4]])
                        free["on", half] = [t]
                    src = psum[:, 3:5, :].rearrange("p w (r h) -> p h (w r)", h=32)[:, 0:H, :]
                    dst = ot[pr % 2][:, :, :].rearrange("p b (h d) -> p h b d", h=H)
                    t = dve(lambda e: e.transpose(dst, src), [t, *free.get(("ot", pr % 2), [])])
                    bank_read[3] = bank_read[4] = [t]
                    ready["ot", pr] = [t]

                def tokens_attend(s):
                    for c in range(4 * s, 4 * s + 4 if s < B else 4 * s + 1):
                        if c == 0:
                            expand(0)
                        if c < 4 * B:
                            scores(c)
                            yield
                        if c:
                            turn_probs(c - 1)
                            yield
                            attend(c - 1)
                        yield
                        if c + 1 < 4 * B:
                            expand(c + 1)
                        yield
                        if c and c % 2 == 0:
                            turn_out(c // 2 - 1)
                        yield

                def back(s):
                    r, nm = rs[s % 3], negm[s % 3]
                    while ("ot", 2 * s + 1) not in ready:
                        yield
                    hs = []
                    for k in range(KC):
                        b = single()
                        for i in range(NT):
                            pr = 2 * s + i // 2
                            t = pe(lambda e, i=i, pr=pr, k=k, b=b: e.transpose(
                                psum[:, b, i * P:(i + 1) * P], ot[pr % 2][:, i % 2, k * P:(k + 1) * P], ident[:, :]),
                                [*ready["ot", pr], *bank_read[b]])
                        hi, lo = oT[:, 0, k, :], oT[:, 1, k, :]
                        th = act(lambda e, hi=hi, b=b: e.activation(hi, psum[:, b, :], ACT.Copy), [t, *free.get("oT", [])])
                        tl = dve(lambda e, hi=hi, lo=lo, b=b: e.tensor_tensor(lo, psum[:, b, :], hi.bitcast(F32), ALU.subtract), [th])
                        bank_read[b] = [tl]
                        hs += [th, tl]
                    free["ot", 0] = free["ot", 1] = [t]
                    for i in range(NT):
                        tx = pool(lambda e, i=i: e.tensor_scalar(x1[:, i, :], X[:, s, i, :], r[:, 0, i:i + 1], nm[:, 1, i:i + 1],
                                                                 ALU.mult, ALU.add), [ready["rs", s], *free.get("x1", [])])
                    yield
                    for p in range(NT // 2):
                        b = single()
                        for i in (2 * p, 2 * p + 1):
                            t = product(psum[:, b, (i % 2) * D:(i % 2 + 1) * D], three(oT, i, wo), [*hs, *bank_read[b]], BO, D)
                        v = x1[:, 2 * p:2 * p + 2, :].rearrange("p i d -> p (i d)")
                        t = dve(lambda e, v=v, b=b: e.tensor_tensor(v, psum[:, b, :], v, ALU.add), [t, tx])
                        bank_read[b] = [t]
                        for i in (2 * p, 2 * p + 1):
                            tq = act(lambda e, i=i: e.activation(xs2[:, i, :], x1[:, i, :], ACT.Square,
                                                                 accum_out=ssq[s % 2][:, i:i + 1]), [t, *free.get("xs2", [])])
                        yield
                    free["oT"] = [(s_pe, s_pe.count)]
                    q = rms[s % 2]
                    tp = pool(lambda e: e.tensor_scalar(q[:, :], ssq[s % 2][:, :], 1.0 / D, RMS_EPS, ALU.mult, ALU.add), [tq])
                    tp = pool(lambda e: e.tensor_tensor(q[:, :], q[:, :], half_neg[:, 0:NT], ALU.pow), [tp])
                    xv = X[:, s].rearrange("p i d -> p (i d)")
                    t = dve(lambda e: e.scalar_tensor_tensor(out=xv, in0=x1[:, :, :].rearrange("p i d -> p (i d)"), scalar=0.5,
                                                             in1=xv, op0=ALU.mult, op1=ALU.add), [t])
                    ready["x", s] = t
                    yield
                    for i in range(NT):
                        ta = act(lambda e, i=i: e.activation(xs2[:, i, :], x1[:, i, :], ACT.Copy, scale=q[:, i:i + 1]), [tp])
                    free["x1"] = [t, ta]
                    yield
                    hs = []
                    for k in range(KC):
                        tt, tp_ = transposed_split(xs2, h2[s % 2], single(), k, gam[:, 1, k:k + 1], [ta], free.get(("h2", s % 2), []))
                        hs += tt
                        free["xs2"] = [tp_]
                        yield
                    ready["h2", s] = hs
                    b = single()
                    for i in range(NT):
                        t = product(psum[:, b, i * E:(i + 1) * E], three(h2[s % 2], i, wg), [*hs, *bank_read[b]], BG, E)
                    pg = psum[:, b, 0:NT * E].rearrange("p (i e) -> p i e", e=E)
                    g = gate[s % 2]
                    wide = lambda n: gs[:, n, :].unsqueeze(2).to_broadcast([P, NT, E])
                    t = dve(lambda e: e.tensor_reduce(gs[:, 0, :], pg, AX.X, ALU.max), [t])
                    t = dve(lambda e: e.tensor_tensor(gl[:, :, :], pg, wide(0), ALU.subtract), [t])
                    bank_read[b] = [t]
                    yield
                    t = act(lambda e: e.activation(gl[:, :, :], gl[:, :, :], ACT.Exp), [t])
                    t = dve(lambda e: e.tensor_reduce(gs[:, 1, :], gl[:, :, :], AX.X, ALU.add), [t])
                    t = dve(lambda e: e.reciprocal(gs[:, 2, :], gs[:, 1, :]), [t])
                    t = dve(lambda e: e.tensor_scalar(gs[:, 0, :], gs[:, 2, :], 0.5, None, ALU.mult), [t])
                    t = dve(lambda e: e.tensor_tensor(g[:, :, :], gl[:, :, :], wide(0), ALU.mult), [t, *free.get(("gate", s % 2), [])])
                    ready["gate", s] = t
                    yield

                def experts(s):
                    g, h = gate[s % 2], h2[s % 2]
                    done = []
                    for i in range(NT):
                        xi = X[:, s, i, :]
                        tv, ty = ready["x", s], []
                        for n, ep in enumerate((0, 1, 2, 3)):
                            b = turn[1] % 3
                            turn[1] += 1
                            t = product(psum[:, b, :], [(l, w) for l, w in three(h, i, we[:, :, :, 2 * ep:2 * ep + 2, :])],
                                        [*t_we, *ready["h2", s], *bank_read[b]])
                            for u in range(2):
                                e_ = 2 * ep + u
                                ps, gc = psum[:, b, u * D:(u + 1) * D], g[:, i, e_:e_ + 1]
                                if ep % 2 == 0:
                                    tr = tv = dve(lambda e, ps=ps, gc=gc, xi=xi: e.scalar_tensor_tensor(
                                        out=xi, in0=ps, scalar=gc, in1=xi, op0=ALU.mult, op1=ALU.add), [t, tv, ready["gate", s]])
                                else:
                                    slot = ep // 2 * 2 + u
                                    tr = act(lambda e, ps=ps, gc=gc, slot=slot: e.activation(y[:, slot, :], ps, ACT.Copy, scale=gc),
                                             [t, ready["gate", s], *free.get("y", [])])
                                    ty = [tr]
                            bank_read[b] = [tr]
                            yield
                        ta = pool(lambda e: e.tensor_tensor(y[:, 0:2, :], y[:, 0:2, :], y[:, 2:4, :], ALU.add), ty)
                        ta = pool(lambda e: e.tensor_tensor(y[:, 0, :], y[:, 0, :], y[:, 1, :], ALU.add), [ta])
                        ta = pool(lambda e, xi=xi: e.tensor_tensor(xi, xi, y[:, 0, :], ALU.add), [ta, tv])
                        free["y"] = [ta]
                        done.append(ta)
                    free["h2", s % 2] = [t]
                    free["gate", s % 2] = [tv, tr]
                    x_ready[s] = [done[-1]]

                for step in range(B + 3):
                    interleave(
                        (experts(step - 3), 4 * NT) if 0 <= step - 3 else (None, 1),
                        (back(step - 2), 10) if 0 <= step - 2 < B else (None, 1),
                        (tokens_attend(step - 1), 20) if 0 <= step - 1 <= B else (None, 1),
                        (front(step), 9) if step < B else (None, 1),
                    )
                    if tag == "b" and 0 <= step - 3 < B:
                        b = step - 3
                        SP.do(lambda e, b=b: e.dma_start(out[b].rearrange("(p i) d -> p i d", i=NT), X[:, b, :, :]),
                              x_ready[b], s_out)
                if tag == "b":
                    SP.hold(s_out, 16 * B)
                with nc.Block() as block:
                    _issue(block, PE, DVE, SCA, POOL, SP)

        def attention():
            NQ = S // 2
            HH = G // 2
            EXR = 4
            with ExitStack() as scope:
                def sb(name, shape, dt=F32):
                    return sbt(scope, f"{name}_s", shape, dt)

                aw = [sb(f"aw{n}", [P, 2, KC, D], F32R) for n in range(3)]
                neg_id = sb("neg_id", [P, P], F32R)
                raw = sb("bn_raw", [P, NT, 6])
                mv = sb("mv", [P, NT, 2])
                rs = sb("rs", [P, 4, NT])
                xs = sb("xs", [P, NT, D])
                hT = sb("hT", [P, 2, KC, S], F32R)
                parts = [sb(f"part{n}", [P, 2, S], F32R) for n in range(2)]
                qs = [sb(f"qs{n}", [3 * GD, G, S], F32R) for n in range(2)]
                ks = [sb(f"ks{n}", [3 * GD, G, S], F32R) for n in range(2)]
                v = [sb(f"v{n}", [P, NT, D]) for n in range(2)]
                first = [sb(f"first{n}", [P, HH, NQ]) for n in range(2)]
                tree = sb("tree", [P, HH, NQ])
                mr = [sb(f"mr{n}", [P, NQ], F32R) for n in range(2)]
                ex = [sb(f"ex{n}", [P, G, NQ]) for n in range(EXR)]
                rec = [sb(f"rec{n}", [P, NQ]) for n in range(2)]
                ct = sb("ct", [P, NHG, NQ])
                s_aw = [sem(f"s_aw{n}", 16) for n in range(3)]
                s_st = [sem(f"s_st{n}", 16) for n in range(12)]

                aw_raw = ex[0][:, 0:6, :].rearrange("p (n k) d -> p n k d", n=3)
                for n, name in enumerate(("Wq", "Wk", "Wv")):
                    t = SP.do(lambda e, n=n, name=name: e.dma_start(
                        aw_raw[:, n], a[f"L0_attn_{name}"].rearrange("(k c) n -> c k n", c=P)), (), s_aw[n])
                    th = act(lambda e, n=n: e.activation(aw[n][:, 0], aw_raw[:, n], ACT.Copy), [t])
                    t_aw = dve(lambda e, n=n: e.tensor_tensor(aw[n][:, 1], aw_raw[:, n], aw[n][:, 0].bitcast(F32), ALU.subtract), [th])
                t_neg = dve(lambda e: e.tensor_scalar(neg_id[:, :], ident[:, :], -1.0, None, ALU.mult))
                free, ready = {("ex", 0): [t_aw]}, {}

                def front(b):
                    for i in range(NT):
                        t = dve(lambda e, i=i: e.bn_stats(raw[:, i, :], X[:, b, i, :]), x_ready[b])
                        t = dve(lambda e, i=i: e.bn_aggr(mv[:, i, :], raw[:, i, :]), [t])
                        if i % 2:
                            yield
                    t = pool(lambda e: e.tensor_scalar(rs[:, 1, :], mv[:, :, 1], LN_EPS, None, ALU.add), [t])
                    t = pool(lambda e: e.tensor_tensor(rs[:, 0, :], rs[:, 1, :], half_neg[:, 0:NT], ALU.pow), [t])
                    for i in range(NT):
                        tx = dve(lambda e, i=i: e.tensor_scalar(xs[:, i, :], X[:, b, i, :], mv[:, i, 0:1], rs[:, 0, i:i + 1],
                                                                ALU.subtract, ALU.mult), [t, *free.get("xs", [])])
                        if i % 2:
                            yield
                    hs = []
                    for k in range(KC):
                        tt, tp = transposed_split(xs, hT, 7, k, 1.0, [tx], free.get("hT", []))
                        hs += tt
                        free["xs"] = [tp]
                        yield
                    stacked = []

                    def queries_or_keys(slot):
                        w, dst, hg = ((1, ks[b % 2], slot), (0, qs[b % 2], slot - NHG))[slot // NHG]
                        terms = [(aw[w][:, y_, k, hg * P:(hg + 1) * P], hT[:, x_, k, :])
                                 for k in range(KC) for x_, y_ in ((0, 0), (1, 0), (0, 1))]
                        t = product(psum[:, 7, :], terms, [t_aw, *hs, *bank_read[7]])
                        n = slot % 2
                        hi, lo, bc = parts[n][:, 0, :], parts[n][:, 1, :], abq[:, w, hg:hg + 1]
                        th = act(lambda e: e.activation(hi, psum[:, 7, :], ACT.Identity, bias=bc), [t, *free.get(("part", n), [])])
                        tl = dve(lambda e: e.scalar_tensor_tensor(out=lo, in0=psum[:, 7, :], scalar=bc, in1=hi.bitcast(F32),
                                                                  op0=ALU.add, op1=ALU.subtract), [th])
                        bank_read[7] = [tl]
                        toks = []
                        for row, x_ in enumerate((0, 0, 1) if w == 0 else (0, 1, 0)):
                            for h in range(HQ):
                                tt = SP.do(lambda e, row=row, x_=x_, h=h: e.dma_start(
                                    dst[row * GD:(row + 1) * GD, hg * HQ + h, :].bitcast(F32),
                                    parts[n][h * GD:(h + 1) * GD, x_, :].bitcast(F32)),
                                    [th, tl, *free.get(("stack", b % 2), [])], s_st[slot * 3 + row])
                            toks.append(tt)
                        free["part", n] = toks
                        stacked.extend(toks)

                    def values_of(tiles):
                        n = len(tiles) * D
                        for c, i in enumerate(tiles):
                            t = product(psum[:, 7, c * D:(c + 1) * D], three(hT, i, aw[2]), [*hs, *bank_read[7]], BV, D)
                        t = act(lambda e: e.activation(v[b % 2][:, tiles[0]:tiles[-1] + 1, :].rearrange("p i d -> p (i d)"),
                                                       psum[:, 7, 0:n], ACT.Copy), [t, *free.get(("v", b % 2), [])])
                        bank_read[7] = [t]
                        ready["v", b] = t

                    for piece, n in ((queries_or_keys, 0), (values_of, [0]), (queries_or_keys, 1), (values_of, [1]),
                                     (queries_or_keys, 2), (values_of, [2, 3]), (queries_or_keys, 3)):
                        piece(n)
                        yield
                    free["hT"] = [(s_pe, s_pe.count)]
                    ready["stack", b] = stacked

                def of(u):
                    return u // (2 * NT), u // NT % 2, u % NT

                def half_banks(u, half):
                    return 2 * ((2 * u + half) % 3)

                def score(u, half):
                    b, nq, m = of(u)
                    b0 = half_banks(u, half)
                    for g in range(HH):
                        h = half * HH + g
                        dst = psum[:, b0 + g // 2, (g % 2) * NQ:(g % 2 + 1) * NQ]
                        t = pe(lambda e, h=h, dst=dst: e.matmul(dst, ks[b % 2][:, h, m * P:(m + 1) * P],
                                                                qs[b % 2][:, h, nq * NQ:(nq + 1) * NQ],
                                                                start=(h % 2 == 0), stop=False, skip_group_check=True),
                               [*ready["stack", b], *bank_read[b0], *bank_read[b0 + 1]])
                    ready["score", u, half] = t
                    if half and nq == 1 and m == NT - 1:
                        free["stack", b % 2] = [t]

                def heads(u, half):
                    b0 = half_banks(u, half)
                    return psum[:, b0:b0 + 2, :].rearrange("p k (g n) -> p (k g) n", g=2)

                def copy_first(u):
                    t = act(lambda e: e.activation(first[u % 2][:, :, :], heads(u, 0), ACT.Copy),
                            [ready["score", u, 0], *free.get(("first", u % 2), [])])
                    ready["first", u] = t

                def maximum(u):
                    t = dve(lambda e: e.tensor_tensor(tree[:, :, :], heads(u, 1), first[u % 2][:, :, :], ALU.max),
                            [ready["first", u], ready["score", u, 1], *free.get("tree", [])])
                    free["first", u % 2] = [t]
                    t = dve(lambda e: e.tensor_tensor(tree[:, 0:2, :], tree[:, 0:2, :], tree[:, 2:4, :], ALU.max), [t])
                    t = dve(lambda e: e.tensor_tensor(mr[u % 2][:, :], tree[:, 0, :], tree[:, 1, :], ALU.max),
                            [t, *free.get(("mr", u % 2), [])])
                    ready["max", u] = t
                    free["tree"] = [t]

                def shift(u, half):
                    b0 = half_banks(u, half)
                    for g in range(HH):
                        dst = psum[:, b0 + g // 2, (g % 2) * NQ:(g % 2 + 1) * NQ]
                        t = pe(lambda e, dst=dst: e.matmul(dst, neg_id[:, :], mr[u % 2][:, :], start=False, stop=True,
                                                           skip_group_check=True), [ready["max", u], t_neg])
                    te = act(lambda e: e.activation(ex[u % EXR][:, half * HH:(half + 1) * HH, :], heads(u, half), ACT.Exp,
                                                    scale=float(D) ** -0.5), [t, *free.get(("ex", u % EXR), [])])
                    bank_read[b0] = bank_read[b0 + 1] = [te]
                    free["mr", u % 2] = [t]
                    ready["ex", u] = [te]

                def total(u):
                    e_ = ex[u % EXR]
                    t = dve(lambda e: e.tensor_tensor(tree[:, :, :], e_[:, 0:4, :], e_[:, 4:8, :], ALU.add),
                            [*ready["ex", u], *free.get("tree", [])])
                    t = dve(lambda e: e.tensor_tensor(tree[:, 0:2, :], tree[:, 0:2, :], tree[:, 2:4, :], ALU.add), [t])
                    r = rec[u % 2]
                    t = dve(lambda e: e.tensor_tensor(r[:, :], tree[:, 0, :], tree[:, 1, :], ALU.add), [t, *free.get(("rec", u % 2), [])])
                    ready["total", u] = t
                    free["tree"] = [t]

                def inverse(u):
                    r = rec[u % 2]
                    t = act(lambda e: e.activation(r[:, :], r[:, :], ACT.Ln), [ready["total", u]])
                    t = act(lambda e: e.activation(r[:, :], r[:, :], ACT.Exp, scale=-1.0), [t])
                    ready["inverse", u] = t

                def normalise(u):
                    e_, r = ex[u % EXR], rec[u % 2]
                    by = lambda n: r[:, :].unsqueeze(1).to_broadcast([P, n, NQ])
                    done = [pool(lambda e: e.tensor_tensor(e_[:, 0:MG, :], e_[:, 0:MG, :], by(MG), ALU.mult), [ready["inverse", u]])]
                    if MG < G:
                        done.append(dve(lambda e: e.tensor_tensor(e_[:, MG:G, :], e_[:, MG:G, :], by(G - MG), ALU.mult),
                                        [ready["inverse", u]]))
                    free["rec", u % 2] = done
                    ready["probs", u] = done

                def values(u):
                    b, nq, m = of(u)
                    for hg in range(NHG):
                        for j in range(HQ):
                            h = hg * HQ + j
                            t = pe(lambda e, h=h, j=j, hg=hg: e.matmul(
                                psum[32 * j:32 * j + 32, 6, hg * NQ:(hg + 1) * NQ], v[b % 2][:, m, h * GD:(h + 1) * GD],
                                ex[u % EXR][:, h, :], start=(m == 0 and hg == 0), stop=(m == NT - 1), skip_group_check=True),
                                [ready["v", b], *ready["probs", u], *(bank_read[6] if m == 0 else ())])
                    free["ex", u % EXR] = [t]
                    if m < NT - 1:
                        return
                    if nq == 1:
                        free["v", b % 2] = [t]
                    tc = act(lambda e: e.activation(ct[:, :, :].rearrange("p g n -> p (g n)"), psum[:, 6, :], ACT.Copy),
                             [t, *free.get("ct", [])])
                    bank_read[6] = [tc]
                    ready["ct"] = tc

                def finish(u):
                    b, nq, m = of(u)
                    if m < NT - 1:
                        return
                    ni = NQ // P
                    for i in range(ni):
                        for hg in range(NHG):
                            t = pe(lambda e, i=i, hg=hg: e.transpose(psum[:, 7, (i * NHG + hg) * P:(i * NHG + hg + 1) * P],
                                                                     ct[:, hg, i * P:(i + 1) * P], ident[:, :]),
                                   [ready["ct"], *bank_read[7]])
                    free["ct"] = [t]
                    xv = X[:, b, nq * ni:(nq + 1) * ni, :].rearrange("p i d -> p (i d)")
                    t = dve(lambda e: e.tensor_tensor(xv, psum[:, 7, :], xv, ALU.add), [t])
                    bank_read[7] = [t]
                    x_ready[b] = [t]

                units = 2 * NT * B
                for _ in front(0):
                    pass
                ahead = front(1)
                for _ in range(4):
                    next(ahead)
                score(0, 0)
                copy_first(0)
                for u in range(units + 4):
                    b, it = u // (2 * NT), u % (2 * NT)
                    places = ("b", "b", "c", "bc", "bc", "bc", "ab", "ab")[it]
                    if it == 2 * NT - 2:
                        for _ in ahead:
                            pass
                        ahead = front(b + 2) if b + 2 < B else iter(())
                    if 0 <= u - 1 < units:
                        shift(u - 1, 0)
                        shift(u - 1, 1)
                    if "a" in places:
                        next(ahead, None)
                    if 0 <= u - 2 < units:
                        inverse(u - 2)
                    if u < units:
                        score(u, 1)
                        maximum(u)
                    if "b" in places:
                        next(ahead, None)
                    if u + 1 < units:
                        score(u + 1, 0)
                        copy_first(u + 1)
                    if "c" in places:
                        next(ahead, None)
                    if 0 <= u - 1 < units:
                        total(u - 1)
                    if 0 <= u - 2 < units:
                        normalise(u - 2)
                    if 0 <= u - 4 < units:
                        finish(u - 4)
                    if 0 <= u - 3 < units:
                        values(u - 3)
                with nc.Block() as block:
                    _issue(block, PE, DVE, SCA, POOL, SP)

        ffn("a")
        attention()
        ffn("b")


MG = 8
EXPAND = "VPVAVPVA"


def _issue(block, pe_lane, dve_lane, act_lane, pool_lane, sp_lane):
    @block.tensor
    def _(e):
        pe_lane.issue(e)

    @block.vector
    def _(e):
        dve_lane.issue(e)

    @block.scalar
    def _(e):
        act_lane.issue(e)

    @block.gpsimd
    def _(e):
        pool_lane.issue(e)

    @block.sync
    def _(e):
        sp_lane.issue(e)


_INS = ["L0_attn_hidden_states", "L0_attn_Wq", "L0_attn_bq", "L0_attn_Wk", "L0_attn_bk", "L0_attn_Wv", "L0_attn_bv",
        "L0_ffn_gamma1", "L0_ffn_Wq", "L0_ffn_bq", "L0_ffn_Wdown", "L0_ffn_bdown", "L0_ffn_Wup", "L0_ffn_bup",
        "L0_ffn_Wo", "L0_ffn_bo", "L0_ffn_gamma2", "L0_ffn_Wg", "L0_ffn_bg", "L0_ffn_We"]


def kernel(**inputs):
    import numpy as _np
    import concourse.bacc as _bacc
    from concourse.bass_utils import run_bass_kernel_spmd as _run

    nc = _bacc.Bacc("TRN2", target_bir_lowering=False, num_devices=1)
    arrays, aps = {}, {}
    for name in _INS:
        v = _np.ascontiguousarray(inputs[name])
        arrays[f"in_{name}"] = v
        aps[name] = nc.dram_tensor(f"in_{name}", v.shape, mybir.dt.from_np(v.dtype), kind="ExternalInput").ap()
    shape = arrays["in_L0_attn_hidden_states"].shape
    out = nc.dram_tensor("out", shape, F32, kind="ExternalOutput").ap()
    macaron(nc, aps, out)
    r = _run(nc, [arrays], core_ids=[0])
    return r.results[0]["out"]
```

```python
from contextlib import ExitStack

import concourse.bass as bass
from concourse import mybir

F32 = mybir.dt.float32
F32R = mybir.dt.float32r
ALU = mybir.AluOpType
ACT = mybir.ActivationFunctionType
AX = mybir.AxisListType

P = 128
BANK = 512
LN_EPS = 1e-5
RMS_EPS = 1e-6


class Signal:

    def __init__(self, sem, step=1):
        self.sem, self.step, self.count = sem, step, 0

    def next(self):
        self.count += self.step
        return (self, self.count)


class Lane:

    def __init__(self):
        self.items = []

    def do(self, emit, after=(), done=None):
        value = done.next() if done is not None else None
        self.items.append((emit, tuple(after), value))
        return value

    def hold(self, sig, value):
        self.items.append((None, ((sig, value),), None))

    def issue(self, eng):
        passed = {}
        for emit, after, value in self.items:
            for sig, need in after:
                if passed.get(id(sig), 0) < need:
                    eng.wait_ge(sig.sem, need)
                    passed[id(sig)] = need
            if emit is None:
                continue
            ins = emit(eng)
            if value is not None:
                ins.then_inc(value[0].sem, value[0].step)
        self.items = []


def interleave(*lists):
    live = [[g, n, 0] for g, n in lists if g is not None]
    while live:
        live.sort(key=lambda x: x[2] / x[1])
        g = live[0]
        g[2] += 1
        try:
            next(g[0])
        except StopIteration:
            live.pop(0)


def macaron(nc, a, out):
    x_dram = a["L0_attn_hidden_states"]
    B, S, D = x_dram.shape
    NT = S // P
    KC = D // P
    L = a["L0_ffn_Wdown"].shape[1]
    E = a["L0_ffn_We"].shape[0]
    H, HD = 16, D // 16
    G = 8
    GD = D // G
    T8 = P // HD
    NR = 32
    CR = NR // 2
    HQ = P // GD
    NHG = G // HQ
    assert S == BANK and KC == 2 and 2 * L == P and T8 == 8 and HD == 16 and HQ == 4

    ctx = ExitStack()
    with ctx:
        def sem(name, step=1):
            return Signal(ctx.enter_context(nc.semaphore(name)), step)

        def sbt(scope, name, shape, dt=F32):
            return scope.enter_context(nc.sbuf_tensor(name, shape, dt))

        PE, DVE, SCA, POOL, SP = Lane(), Lane(), Lane(), Lane(), Lane()

        s_pe, s_dve, s_act, s_pool = sem("s_pe"), sem("s_dve"), sem("s_act"), sem("s_pool")
        s_x = [sem(f"s_x{b}", 16) for b in range(B)]
        s_w = [sem(f"s_w{n}", 16) for n in range(30)]
        s_out = sem("s_out", 16)

        def pe(emit, after=()):
            return PE.do(emit, after, s_pe)

        def dve(emit, after=()):
            return DVE.do(emit, after, s_dve)

        def act(emit, after=()):
            return SCA.do(emit, after, s_act)

        def pool(emit, after=()):
            return POOL.do(emit, after, s_pool)

        psum = ctx.enter_context(nc.psum_tensor("psum", [P, 8, BANK], F32))
        bank_read = [[] for _ in range(8)]

        X = sbt(ctx, "X", [P, B, NT, D])
        ident = sbt(ctx, "ident", [P, P])
        mask8 = sbt(ctx, "mask8", [P, T8])
        half_neg = sbt(ctx, "half_neg", [P, 8])
        row1 = sbt(ctx, "row1", [2, 1])
        ones2f = sbt(ctx, "ones2f", [2, P])
        ones2 = sbt(ctx, "ones2", [2, P], F32R)
        wq = sbt(ctx, "wq", [P, 2, KC, D], F32R)
        wo = sbt(ctx, "wo", [P, 2, KC, D], F32R)
        wd = sbt(ctx, "wd", [P, 2, KC, 2 * L], F32R)
        wu = sbt(ctx, "wu", [P, 2, 2 * D], F32R)
        wg = sbt(ctx, "wg", [P, 2, KC, E], F32R)
        NB = D + 2 * D + D + D
        BQ, BU, BO, BV = 0, D, 3 * D, 4 * D
        bias = sbt(ctx, "bias", [2, NB], F32R)
        gam = sbt(ctx, "gam", [P, 2, KC])
        bdn = sbt(ctx, "bdn", [P, 1])
        bgate = sbt(ctx, "bgate", [E, 1])
        abq = sbt(ctx, "abq", [P, 2, KC])

        n_w = [0]

        def load(dst, src, columns=False):
            s = s_w[n_w[0]]
            n_w[0] += 1
            return SP.do(lambda e: e.dma_start(dst, src, allow_slow_non_contiguous=columns), (), s)

        def load_x(b):
            SP.do(lambda e: e.dma_start(X[:, b, :, :], x_dram[b].rearrange("(p i) d -> p i d", i=NT)), (), s_x[b])

        load_x(0)
        SCA.do(lambda e: e.preload_act_table_set("natural_log_exp_and_others"))
        t = pool(lambda e: e.memset(ident[:, :], 0.0))
        t_id = pool(lambda e: e.affine_select(out=ident[:, :], in_=ident[:, :], compare_op=ALU.not_equal, fill=1.0,
                                              base=0, pattern=[[-1, P]], channel_multiplier=1), [t])
        t_half = pool(lambda e: e.memset(half_neg[:, :], -0.5))
        t_1 = pool(lambda e: e.memset(ones2f[:, :], 1.0))
        t_mask = dve(lambda e: e.tensor_reduce(mask8[:, :], ident[:, :].rearrange("p (t c) -> p t c", t=T8), AX.X, ALU.add), [t_id])
        t_row1 = dve(lambda e: e.tensor_copy(row1[:, :], ident[0:2, 1:2]), [t_id])
        t_ones = dve(lambda e: e.tensor_copy(ones2[:, :], ones2f[:, :]), [t_1])
        made = {"ident": [t_id], "half_neg": [t_half], "mask8": [t_mask], "ones2": [t_ones]}

        def load_weights(stage, stage_hi):
            at = [0]

            def piece(rows, *shape):
                n = 1
                for d in shape:
                    n *= d
                v = stage[0:rows, at[0]:at[0] + n]
                at[0] += n
                return v

            def split(dst_hi, dst_lo, src, landed):
                th = act(lambda e: e.activation(dst_hi, src, ACT.Copy), landed)
                return [dve(lambda e: e.tensor_tensor(dst_lo, src, dst_hi.bitcast(F32), ALU.subtract), [th, *landed])]

            raw_d = piece(P, KC, 2, L).rearrange("p (k r l) -> p k r l", k=KC, r=2)
            raw_q, raw_o = (piece(P, KC, D).rearrange("p (k n) -> p k n", k=KC) for _ in range(2))
            raw_u = piece(P, 2 * D)
            raw_g = piece(P, KC, E).rearrange("p (k n) -> p k n", k=KC)
            raw_b, bhi = piece(2, NB), stage_hi[0:2, 0:NB]
            t_d = [load(raw_d[:, :, r, :], a["L0_ffn_Wdown"].rearrange("(k c) n -> c k n", c=P)) for r in range(2)]
            made["gam1"] = [load(gam[:, 0, :], a["L0_ffn_gamma1"].rearrange("(k c) -> c k", c=P), True)]
            made["bdn"] = [load(bdn[r * L:(r + 1) * L, :], a["L0_ffn_bdown"].rearrange("(n o) -> n o", o=1)) for r in range(2)]
            t_q = load(raw_q, a["L0_ffn_Wq"].rearrange("(k c) n -> c k n", c=P))
            t_b = []
            for at_, name in ((BQ, "L0_ffn_bq"), (BU, "L0_ffn_bup"), (BO, "L0_ffn_bo"), (BV, "L0_attn_bv")):
                src = a[name]
                for r in range(2):
                    t_b.append(load(raw_b[r:r + 1, at_:at_ + src.shape[0]], src.rearrange("(o n) -> o n", o=1)))
            t_u = [load(raw_u[r * L:(r + 1) * L, :], a["L0_ffn_Wup"]) for r in range(2)]
            load_x(1)
            t_o = load(raw_o, a["L0_ffn_Wo"].rearrange("(k c) n -> c k n", c=P))
            t_g = load(raw_g, a["L0_ffn_Wg"].rearrange("(k c) n -> c k n", c=P))
            made["gam2"] = [load(gam[:, 1, :], a["L0_ffn_gamma2"].rearrange("(k c) -> c k", c=P), True)]
            made["bgate"] = [load(bgate[:, :], a["L0_ffn_bg"].rearrange("(n o) -> n o", o=1))]
            made["abq"] = [load(abq[:, n, :], a[name].rearrange("(k c) -> c k", c=P), True)
                           for n, name in enumerate(("L0_attn_bq", "L0_attn_bk"))]
            for b in range(2, B):
                load_x(b)

            def early():
                made["wd"] = split(wd[:, 0], wd[:, 1], raw_d.rearrange("p k r l -> p k (r l)"), t_d)
                made["wq"] = split(wq[:, 0], wq[:, 1], raw_q, [t_q])
                t = act(lambda e: e.activation(bhi.bitcast(F32R), raw_b, ACT.Copy), t_b)
                t = dve(lambda e: e.tensor_scalar(bhi.bitcast(F32R), bhi, row1[:, 0:1], None, ALU.mult), [t, t_row1])
                made["bias"] = [dve(lambda e: e.tensor_tensor(bias[:, :], raw_b, bhi, ALU.subtract), [t, *t_b])]
                made["wu"] = split(wu[:, 0], wu[:, 1], raw_u, t_u)

            def late():
                made["wo"] = split(wo[:, 0], wo[:, 1], raw_o, [t_o])
                made["wg"] = split(wg[:, 0], wg[:, 1], raw_g, [t_g])
                return made["wg"]

            return early, late

        def transposed_split(src, hl, bank, k, gamma, ready, hl_free):
            for i in range(NT):
                t = pe(lambda e, i=i: e.transpose(psum[:, bank, i * P:(i + 1) * P], src[:, i, k * P:(k + 1) * P], ident[:, :]),
                       [*made["ident"], *ready, *bank_read[bank]])
            hi, lo, ps = hl[:, 0, k, :], hl[:, 1, k, :], psum[:, bank, :]
            th = act(lambda e: e.activation(hi, ps, ACT.Copy, scale=gamma), [t, *hl_free])
            tl = dve(lambda e: e.scalar_tensor_tensor(out=lo, in0=ps, scalar=gamma, in1=hi.bitcast(F32),
                                                      op0=ALU.mult, op1=ALU.subtract), [th])
            bank_read[bank] = [tl]
            return [th, tl], t

        def product(out_ap, terms, after, bias_at=None, width=0):
            if bias_at is not None:
                terms = [*terms, (ones2[:, :], bias[:, bias_at:bias_at + width])]
                after = [*after, *made["ones2"], *made["bias"]]
            for n, (l, r) in enumerate(terms):
                t = pe(lambda e, l=l, r=r, n=n: e.matmul(out_ap, l, r, start=(n == 0), stop=(n == len(terms) - 1)),
                       after if n == 0 else ())
            return t

        def three(hl, i, w):
            cols = slice(i * P, (i + 1) * P)
            return [(hl[:, x, k, cols], w[:, y, k]) for k in range(KC) for x, y in ((0, 0), (1, 0), (0, 1))]

        x_ready = [[(s_x[b], 16)] for b in range(B)]

        def ffn(tag):
            with ExitStack() as scope:
                def sb(name, shape, dt=F32):
                    return sbt(scope, f"{name}{tag}", shape, dt)

                raw = sb("bn_raw", [P, NT, 6])
                mv = [sb(f"mv{n}", [P, NT, 2]) for n in range(4)]
                rs = [sb(f"rs{n}", [P, 4, NT]) for n in range(4)]
                xs = sb("xs", [P, NT, D])
                hT = sb("hT", [P, 2, KC, S], F32R)
                la = sb("la", [P, S], F32R)
                qc = [sb(f"qc{n}", [P, NR * H + H]) for n in range(3)]
                kvc = [sb(f"kvc{n}", [P, NR, 2, HD]) for n in range(3)]
                kvx = [sb(f"kvx{n}", [P, CR, 2, T8, HD]) for n in range(2)]
                ex = [sb(f"ex{n}", [P, BANK]) for n in range(2)]
                mx = [sb(f"mx{n}", [P, NR]) for n in range(2)]
                sm = [sb(f"sm{n}", [P, NR]) for n in range(2)]
                rc = [sb(f"rc{n}", [P, NR]) for n in range(3)]
                at = [sb(f"at{n}", [P, CR * H + H]) for n in range(2)]
                on = [sb(f"on{n}", [P, BANK]) for n in range(2)]
                ot = [sb(f"ot{n}", [P, 2, D]) for n in range(2)]
                oT = sb("oT", [P, 2, KC, S], F32R)
                x1 = sb("x1", [P, NT, D])
                xs2 = sb("xs2", [P, NT, D])
                ssq = [sb(f"ssq{n}", [P, NT]) for n in range(2)]
                rms = [sb(f"rms{n}", [P, NT]) for n in range(2)]
                h2 = [sb(f"h2{n}", [P, 2, KC, S], F32R) for n in range(2)]
                gT = sb("gT", [E, S])
                gl = sb("gl", [P, NT, E])
                gs = sb("gs", [P, 3, NT])
                gate = [sb(f"gate{n}", [P, NT, E]) for n in range(2)]
                y = sb("y", [P, 4, D])

                we = sb("we", [P, 2, KC, E, D], F32R)
                negm = [sb(f"negm{n}", [P, 2, NT]) for n in range(4)]
                s_we = [sem(f"s_we{tag}{k}", 16) for k in range(KC)]
                we_raw = [kvx[1][:, k * CR // KC:(k + 1) * CR // KC].rearrange("p r w t d -> p (r w t d)").rearrange(
                    "p (e n) -> p e n", e=E) for k in range(KC)]
                if tag == "a":
                    weights_early, weights_late = load_weights(
                        kvx[0][:, :, :, :, :].rearrange("p r w t d -> p (r w t d)"),
                        h2[1][:, :, :, :].rearrange("p x k t -> p (x k t)").bitcast(F32))
                we_landed = [SP.do(lambda e, k=k: e.dma_start(
                    we_raw[k], a["L0_ffn_We"][:, k * P:(k + 1) * P, :].rearrange("e c n -> c e n")), (), s_we[k]) for k in range(KC)]

                def split_experts():
                    toks = []
                    for k in range(KC):
                        th = act(lambda e, k=k: e.activation(we[:, 0, k], we_raw[k], ACT.Copy), [we_landed[k]])
                        toks.append(dve(lambda e, k=k: e.tensor_tensor(
                            we[:, 1, k], we_raw[k], we[:, 0, k].bitcast(F32), ALU.subtract), [th, we_landed[k]]))
                    made["we"] = free["kvx", 1] = toks

                for q in qc:
                    t_pad = pool(lambda e, q=q: e.memset(q[:, NR * H:], 0.0))
                for q in at:
                    t_pad = pool(lambda e, q=q: e.memset(q[:, CR * H:], 0.0))

                free = {}
                ready = {}
                singles = [5, 6, 7]
                turn = [0, 0]

                def single():
                    turn[0] += 1
                    return singles[turn[0] % 3]

                def norm(s):
                    m, r, nm = mv[s % 4], rs[s % 4], negm[s % 4]
                    for i in range(NT):
                        t = dve(lambda e, i=i: e.bn_stats(raw[:, i, :], X[:, s, i, :]), x_ready[s])
                    for i in range(NT):
                        t = dve(lambda e, i=i: e.bn_aggr(m[:, i, :], raw[:, i, :]), [t])
                    var = m[:, :, 1]
                    t = dve(lambda e: e.tensor_scalar(r[:, 3, :], var, LN_EPS, None, ALU.add), [t])
                    yield
                    t = pool(lambda e: e.tensor_tensor(r[:, 0, :], r[:, 3, :], half_neg[:, 0:NT], ALU.pow),
                             [t, *made["half_neg"]])
                    yield
                    t = dve(lambda e: e.tensor_tensor(r[:, 3, :], var, r[:, 0, :], ALU.mult), [t])
                    t = dve(lambda e: e.tensor_tensor(r[:, 3, :], r[:, 3, :], r[:, 0, :], ALU.mult), [t])
                    t = dve(lambda e: e.tensor_scalar(r[:, 3, :], r[:, 3, :], RMS_EPS, None, ALU.add), [t])
                    t = pool(lambda e: e.tensor_tensor(r[:, 1, :], r[:, 3, :], half_neg[:, 0:NT], ALU.pow), [t])
                    yield
                    t = dve(lambda e: e.tensor_tensor(r[:, 2, :], r[:, 1, :], r[:, 0, :], ALU.mult), [t])
                    for n, of in ((0, 2), (1, 0)):
                        t = dve(lambda e, n=n, of=of: e.scalar_tensor_tensor(
                            out=nm[:, n, :], in0=m[:, :, 0], scalar=-1.0, in1=r[:, of, :], op0=ALU.mult, op1=ALU.mult), [t])
                    ready["rs", s] = t
                    for i in range(NT):
                        t = pool(lambda e, i=i: e.tensor_scalar(xs[:, i, :], X[:, s, i, :], r[:, 2, i:i + 1], nm[:, 0, i:i + 1],
                                                                ALU.mult, ALU.add), [ready["rs", s], *free.get("xs", [])])
                    ready["xs", s] = t

                def front(s):
                    hs = []
                    for k in range(KC):
                        tt, tp = transposed_split(xs, hT, single(), k, gam[:, 0, k:k + 1], [ready["xs", s], *made["gam1"]], free.get("hT", []))
                        hs += tt
                        free["xs"] = [tp]
                        yield
                    b = single()
                    terms = [(wd[:, y_, k, :], hT[:, x_, k, :]) for k in range(KC) for x_, y_ in ((0, 0), (1, 0), (0, 1))]
                    t = product(psum[:, b, :], terms, [*hs, *made["wd"], *bank_read[b]])
                    tm = act(lambda e: e.activation(la[:, :], psum[:, b, :], ACT.Identity, bias=bdn[:, 0:1]), [t, *made["bdn"], *free.get("la", [])])
                    up = slice(L, 2 * L)
                    tl = dve(lambda e: e.scalar_tensor_tensor(out=la[up, :], in0=psum[up, b, :], scalar=bdn[up, 0:1],
                                                              in1=la[up, :].bitcast(F32), op0=ALU.add, op1=ALU.subtract), [tm])
                    bank_read[b] = [tl]
                    yield
                    for p in range(NT // 2):
                        n = (2 * s + p) % 3
                        bq = single()
                        for i in (2 * p, 2 * p + 1):
                            t = product(psum[:, bq, (i % 2) * D:(i % 2 + 1) * D], three(hT, i, wq), [*hs, *made["wq"], *bank_read[bq]], BQ, D)
                        src = psum[:, bq, :].rearrange("p (b h d) -> p h b d", b=2, h=H)
                        dst = qc[n][:, 0:NR * H].rearrange("p (r h) -> p h r", h=H)
                        tq = dve(lambda e, src=src, dst=dst: e.transpose(dst, src), [t, *free.get(("qc", n), [])])
                        bank_read[bq] = [tq]
                        yield
                        for i in (2 * p, 2 * p + 1):
                            terms = [(la[:, i * P:(i + 1) * P], wu[:, y_, :]) for y_ in (0, 1)]
                            bk = 3 + i % 2
                            t = product(psum[:, bk, :], terms, [tl, *made["wu"], *bank_read[3], *bank_read[4]], BU, 2 * D)
                        kv = psum[:, 3:5, :].rearrange("p b (g w d) -> p w b g d", w=2, d=HD)
                        src_k = kv[:, 0].rearrange("p b g d -> p g b d")
                        src_v = kv[:, 1].rearrange("p b g d -> p d b g")
                        fr = [t, *free.get(("kvc", n), [])]
                        dst = kvc[n][:, :, 0, :].rearrange("p r h -> p h r")
                        dve(lambda e, s_=src_k, dst=dst: e.transpose(dst, s_), fr)
                        dst = kvc[n][:, :, 1, :].rearrange("p r h -> p h r")
                        tk = dve(lambda e, s_=src_v, dst=dst: e.transpose(dst, s_), fr)
                        bank_read[3] = bank_read[4] = [tk]
                        ready["qkv", 2 * s + p] = [tq, tk]
                        yield
                    free["hT"] = free["la"] = [t]
                    if s + 1 < B:
                        yield from norm(s + 1)

                def expand(c):
                    pr, half = c // 2, c % 2
                    src = kvc[pr % 3][:, half * CR:(half + 1) * CR, :, :].rearrange("p r w d -> p (r w) d")
                    dst = kvx[c % 2][:, :, :, :, :].rearrange("p r w t d -> p (r w) t d")
                    fr = [*ready["qkv", pr], *made["mask8"], *free.get(("kvx", c % 2), [])]
                    toks = {}
                    for t8 in range(T8):
                        o, m = dst[:, :, t8, :], mask8[:, t8:t8 + 1]
                        who = EXPAND[t8]
                        if who == "V":
                            toks[who] = dve(lambda e, o=o, m=m: e.tensor_scalar(o, src, m, None, ALU.mult), fr)
                        elif who == "A":
                            toks[who] = act(lambda e, o=o, m=m: e.activation(o, src, ACT.Copy, scale=m), fr)
                        else:
                            toks[who] = pool(lambda e, o=o, m=m: e.tensor_scalar(o, src, m, 1.0, ALU.mult, ALU.mult), fr)
                    free["kvc", pr % 3] = [*free.get(("kvc", pr % 3), []), *toks.values()] if half else list(toks.values())
                    ready["kvx", c] = list(toks.values())

                def scores(c):
                    pr, half = c // 2, c % 2
                    b = single()
                    q, kx = qc[pr % 3], kvx[c % 2]
                    for r in range(CR):
                        j, a4 = r % 4, r // 4
                        at0 = (half * CR + r) * H
                        t = pe(lambda e, r=r, j=j, a4=a4, at0=at0: e.matmul(
                            psum[32 * j:32 * j + 32, b, a4 * P:(a4 + 1) * P], q[:, at0:at0 + 32], kx[:, r, 0, :, :],
                            start=True, stop=True), [*ready["kvx", c], *bank_read[b], t_pad])
                    free["qc", pr % 3] = [t]
                    e_, m_, s_, r_ = ex[c % 2], mx[c % 2], sm[c % 2], rc[c % 3]
                    ps = psum[:, b, :].rearrange("p (t g) -> p t g", g=H)
                    ev = e_[:, :].rearrange("p (t g) -> p t g", g=H)
                    t = dve(lambda e: e.tensor_reduce(m_[:, :], ps, AX.X, ALU.max), [t])
                    t = dve(lambda e: e.tensor_tensor(ev, ps, m_[:, :].unsqueeze(2).to_broadcast([P, NR, H]), ALU.subtract),
                            [t, *free.get(("ex", c % 2), [])])
                    bank_read[b] = [t]
                    t = act(lambda e: e.activation(e_[:, :], e_[:, :], ACT.Exp, scale=float(HD) ** -0.5), [t])
                    ready["ex", c] = [t]
                    t = dve(lambda e: e.tensor_reduce(s_[:, :], ev, AX.X, ALU.add), [t])
                    t = dve(lambda e: e.reciprocal(r_[:, :], s_[:, :]), [t])
                    ready["rc", c] = [t]

                def turn_probs(c):
                    b = single()
                    for a4 in range(4):
                        t = pe(lambda e, a4=a4: e.transpose(psum[:, b, a4 * P:(a4 + 1) * P], ex[c % 2][:, a4 * P:(a4 + 1) * P],
                                                            ident[:, :]), [*ready["ex", c], *bank_read[b]])
                    free["ex", c % 2] = [t]
                    src = psum[:, b, :].rearrange("p (r h) -> p r h", h=32)[:, :, 0:H]
                    dst = at[c % 2][:, 0:CR * H].rearrange("p (r h) -> p r h", h=H)
                    t = act(lambda e: e.activation(dst, src, ACT.Copy), [t, *free.get(("at", c % 2), [])])
                    bank_read[b] = [t]
                    ready["at", c] = [t]

                def attend(c):
                    b = single()
                    for r in range(CR):
                        j, a4 = r % 4, r // 4
                        t = pe(lambda e, r=r, j=j, a4=a4: e.matmul(
                            psum[32 * j:32 * j + 32, b, a4 * P:(a4 + 1) * P], at[c % 2][:, r * H:r * H + 32],
                            kvx[c % 2][:, r, 1, :, :], start=True, stop=True), [*ready["at", c], *bank_read[b], t_pad])
                    free["at", c % 2] = free["kvx", c % 2] = [t]
                    ps = psum[:, b, :].rearrange("p (t d) -> p t d", d=HD)
                    ov = on[c % 2][:, :].rearrange("p (t d) -> p t d", d=HD)
                    t = dve(lambda e: e.tensor_tensor(ov, ps, rc[c % 3][:, :].unsqueeze(2).to_broadcast([P, NR, HD]), ALU.mult),
                            [t, *ready["rc", c], *free.get(("on", c % 2), [])])
                    bank_read[b] = [t]
                    ready["on", c] = [t]

                def turn_out(pr):
                    for half in range(2):
                        for a4 in range(4):
                            t = pe(lambda e, a4=a4, half=half: e.transpose(
                                psum[:, 3 + half, a4 * P:(a4 + 1) * P], on[half][:, a4 * P:(a4 + 1) * P], ident[:, :]),
                                [*ready["on", 2 * pr + half], *bank_read[3], *bank_read[4]])
                        free["on", half] = [t]
                    src = psum[:, 3:5, :].rearrange("p w (r h) -> p h (w r)", h=32)[:, 0:H, :]
                    dst = ot[pr % 2][:, :, :].rearrange("p b (h d) -> p h b d", h=H)
                    t = dve(lambda e: e.transpose(dst, src), [t, *free.get(("ot", pr % 2), [])])
                    bank_read[3] = bank_read[4] = [t]
                    ready["ot", pr] = [t]

                def tokens_attend(s):
                    for c in range(4 * s, 4 * s + 4 if s < B else 4 * s + 1):
                        if c == 0:
                            expand(0)
                        if c < 4 * B:
                            scores(c)
                            if c == 0:
                                split_experts()
                            yield
                        if c:
                            turn_probs(c - 1)
                            yield
                            attend(c - 1)
                        yield
                        if c + 1 < 4 * B:
                            expand(c + 1)
                        yield
                        if c and c % 2 == 0:
                            turn_out(c // 2 - 1)
                        yield

                def back(s):
                    r, nm = rs[s % 4], negm[s % 4]
                    while ("ot", 2 * s + 1) not in ready:
                        yield
                    hs = []
                    for k in range(KC):
                        b = single()
                        for i in range(NT):
                            pr = 2 * s + i // 2
                            t = pe(lambda e, i=i, pr=pr, k=k, b=b: e.transpose(
                                psum[:, b, i * P:(i + 1) * P], ot[pr % 2][:, i % 2, k * P:(k + 1) * P], ident[:, :]),
                                [*ready["ot", pr], *bank_read[b]])
                        hi, lo = oT[:, 0, k, :], oT[:, 1, k, :]
                        th = act(lambda e, hi=hi, b=b: e.activation(hi, psum[:, b, :], ACT.Copy), [t, *free.get("oT", [])])
                        tl = dve(lambda e, hi=hi, lo=lo, b=b: e.tensor_tensor(lo, psum[:, b, :], hi.bitcast(F32), ALU.subtract), [th])
                        bank_read[b] = [tl]
                        hs += [th, tl]
                    free["ot", 0] = free["ot", 1] = [t]
                    for i in range(NT):
                        tx = pool(lambda e, i=i: e.tensor_scalar(x1[:, i, :], X[:, s, i, :], r[:, 0, i:i + 1], nm[:, 1, i:i + 1],
                                                                 ALU.mult, ALU.add), [ready["rs", s], *free.get("x1", [])])
                    yield
                    for p in range(NT // 2):
                        b = single()
                        for i in (2 * p, 2 * p + 1):
                            t = product(psum[:, b, (i % 2) * D:(i % 2 + 1) * D], three(oT, i, wo), [*hs, *made["wo"], *bank_read[b]], BO, D)
                        v = x1[:, 2 * p:2 * p + 2, :].rearrange("p i d -> p (i d)")
                        t = dve(lambda e, v=v, b=b: e.tensor_tensor(v, psum[:, b, :], v, ALU.add), [t, tx])
                        bank_read[b] = [t]
                        for i in (2 * p, 2 * p + 1):
                            tq = act(lambda e, i=i: e.activation(xs2[:, i, :], x1[:, i, :], ACT.Square,
                                                                 accum_out=ssq[s % 2][:, i:i + 1]), [t, *free.get("xs2", [])])
                        yield
                    free["oT"] = [(s_pe, s_pe.count)]
                    q = rms[s % 2]
                    tp = dve(lambda e: e.tensor_scalar(q[:, :], ssq[s % 2][:, :], 1.0 / D, RMS_EPS, ALU.mult, ALU.add), [tq])
                    tp = pool(lambda e: e.tensor_tensor(q[:, :], q[:, :], half_neg[:, 0:NT], ALU.pow), [tp])
                    xv = X[:, s].rearrange("p i d -> p (i d)")
                    t = dve(lambda e: e.scalar_tensor_tensor(out=xv, in0=x1[:, :, :].rearrange("p i d -> p (i d)"), scalar=0.5,
                                                             in1=xv, op0=ALU.mult, op1=ALU.add), [t])
                    ready["x", s] = t
                    yield
                    for i in range(NT):
                        ta = act(lambda e, i=i: e.activation(xs2[:, i, :], x1[:, i, :], ACT.Copy, scale=q[:, i:i + 1]), [tp])
                    free["x1"] = [t, ta]
                    yield
                    hs = []
                    for k in range(KC):
                        tt, tp_ = transposed_split(xs2, h2[s % 2], single(), k, gam[:, 1, k:k + 1], [ta, *made["gam2"]], free.get(("h2", s % 2), []))
                        hs += tt
                        free["xs2"] = [tp_]
                        yield
                    ready["h2", s] = hs
                    b = single()
                    terms = [(wg[:, y_, k, :], h2[s % 2][:, x_, k, :]) for k in range(KC) for x_, y_ in ((0, 0), (1, 0), (0, 1))]
                    t = product(psum[0:E, b, :], terms, [*hs, *made["wg"], *bank_read[b]])
                    t = act(lambda e, b=b: e.activation(gT[:, :], psum[0:E, b, :], ACT.Identity, bias=bgate[:, 0:1]),
                            [t, *made["bgate"], *free.get("gT", [])])
                    bank_read[b] = [t]
                    yield
                    b = single()
                    for i in range(NT):
                        t = pe(lambda e, i=i, b=b: e.transpose(psum[:, b, i * E:(i + 1) * E], gT[:, i * P:(i + 1) * P],
                                                               ident[0:E, 0:E]), [t, *bank_read[b]])
                    free["gT"] = [t]
                    pg = psum[:, b, 0:NT * E].rearrange("p (i e) -> p i e", e=E)
                    g = gate[s % 2]
                    wide = lambda n: gs[:, n, :].unsqueeze(2).to_broadcast([P, NT, E])
                    t = dve(lambda e: e.tensor_reduce(gs[:, 0, :], pg, AX.X, ALU.max), [t])
                    t = dve(lambda e: e.tensor_tensor(gl[:, :, :], pg, wide(0), ALU.subtract), [t])
                    bank_read[b] = [t]
                    yield
                    t = act(lambda e: e.activation(gl[:, :, :], gl[:, :, :], ACT.Exp), [t])
                    t = dve(lambda e: e.tensor_reduce(gs[:, 1, :], gl[:, :, :], AX.X, ALU.add), [t])
                    t = dve(lambda e: e.reciprocal(gs[:, 2, :], gs[:, 1, :]), [t])
                    t = dve(lambda e: e.tensor_scalar(gs[:, 0, :], gs[:, 2, :], 0.5, None, ALU.mult), [t])
                    t = dve(lambda e: e.tensor_tensor(g[:, :, :], gl[:, :, :], wide(0), ALU.mult), [t, *free.get(("gate", s % 2), [])])
                    ready["gate", s] = t
                    yield

                def experts(s):
                    g, h = gate[s % 2], h2[s % 2]
                    done = []
                    for i in range(NT):
                        xi = X[:, s, i, :]
                        tv, ty = ready["x", s], []
                        for n, ep in enumerate((0, 1, 2, 3)):
                            b = turn[1] % 3
                            turn[1] += 1
                            t = product(psum[:, b, :], [(l, w) for l, w in three(h, i, we[:, :, :, 2 * ep:2 * ep + 2, :])],
                                        [*made["we"], *ready["h2", s], *bank_read[b]])
                            for u in range(2):
                                e_ = 2 * ep + u
                                ps, gc = psum[:, b, u * D:(u + 1) * D], g[:, i, e_:e_ + 1]
                                if ep % 2 == 0:
                                    tr = tv = dve(lambda e, ps=ps, gc=gc, xi=xi: e.scalar_tensor_tensor(
                                        out=xi, in0=ps, scalar=gc, in1=xi, op0=ALU.mult, op1=ALU.add), [t, tv, ready["gate", s]])
                                else:
                                    slot = ep // 2 * 2 + u
                                    tr = act(lambda e, ps=ps, gc=gc, slot=slot: e.activation(y[:, slot, :], ps, ACT.Copy, scale=gc),
                                             [t, ready["gate", s], *free.get("y", [])])
                                    ty = [tr]
                            bank_read[b] = [tr]
                            yield
                        ta = pool(lambda e: e.tensor_tensor(y[:, 0:2, :], y[:, 0:2, :], y[:, 2:4, :], ALU.add), ty)
                        ta = pool(lambda e: e.tensor_tensor(y[:, 0, :], y[:, 0, :], y[:, 1, :], ALU.add), [ta])
                        ta = pool(lambda e, xi=xi: e.tensor_tensor(xi, xi, y[:, 0, :], ALU.add), [ta, tv])
                        free["y"] = [ta]
                        done.append(ta)
                    free["h2", s % 2] = [t]
                    free["gate", s % 2] = [tv, tr]
                    x_ready[s] = [done[-1]]

                for _ in norm(0):
                    pass
                if tag == "a":
                    weights_early()
                for step in range(B + 3):
                    interleave(
                        (tokens_attend(step - 1), W_TOK) if 0 <= step - 1 <= B else (None, 1),
                        (front(step), W_FRONT) if step < B else (None, 1),
                        (experts(step - 3), 4 * NT) if 0 <= step - 3 else (None, 1),
                        (back(step - 2), W_BACK) if 0 <= step - 2 < B else (None, 1),
                    )
                    if step == 0 and tag == "a":
                        free["kvx", 0] = weights_late()
                    if tag == "b" and 0 <= step - 3 < B:
                        b = step - 3
                        SP.do(lambda e, b=b: e.dma_start(out[b].rearrange("(p i) d -> p i d", i=NT), X[:, b, :, :]),
                              x_ready[b], s_out)
                if tag == "b":
                    SP.hold(s_out, 16 * B)
                with nc.Block() as block:
                    _issue(block, PE, DVE, SCA, POOL, SP)

        def attention():
            NQ = S // 2
            HH = G // 2
            EXR = 3
            with ExitStack() as scope:
                def sb(name, shape, dt=F32):
                    return sbt(scope, f"{name}_s", shape, dt)

                aw = [sb(f"aw{n}", [P, 2, KC, D], F32R) for n in range(3)]
                neg_id = sb("neg_id", [P, P], F32R)
                raw = sb("bn_raw", [P, NT, 6])
                mv = sb("mv", [P, NT, 2])
                rs = sb("rs", [P, 4, NT])
                xs = sb("xs", [P, NT, D])
                hT = sb("hT", [P, 2, KC, S], F32R)
                parts = [sb(f"part{n}", [P, 2, S], F32R) for n in range(3)]
                qs = [sb(f"qs{n}", [3 * GD, G, S], F32R) for n in range(2)]
                ks = [sb(f"ks{n}", [3 * GD, G, S], F32R) for n in range(2)]
                v = [sb(f"v{n}", [P, NT, D]) for n in range(2)]
                first = [sb(f"first{n}", [P, HH, NQ]) for n in range(2)]
                tree = sb("tree", [P, HH, NQ])
                mr = [sb(f"mr{n}", [P, NQ], F32R) for n in range(2)]
                ex = [sb(f"ex{n}", [P, G, NQ]) for n in range(EXR)]
                rec = [sb(f"rec{n}", [P, NQ]) for n in range(2)]
                ct = sb("ct", [P, NHG, NQ])
                s_aw = [sem(f"s_aw{n}", 16) for n in range(3)]
                s_st = [sem(f"s_st{n}", 16) for n in range(12)]

                aw_raw = ex[0][:, 0:6, :].rearrange("p (n k) d -> p n k d", n=3)
                aw_landed = [SP.do(lambda e, n=n, name=name: e.dma_start(
                    aw_raw[:, n], a[f"L0_attn_{name}"].rearrange("(k c) n -> c k n", c=P)), (), s_aw[n])
                    for n, name in enumerate(("Wq", "Wk", "Wv"))]

                def split_weights():
                    for n in (1, 0, 2):
                        th = act(lambda e, n=n: e.activation(aw[n][:, 0], aw_raw[:, n], ACT.Copy), [aw_landed[n]])
                        made["aw", n] = [dve(lambda e, n=n: e.tensor_tensor(aw[n][:, 1], aw_raw[:, n], aw[n][:, 0].bitcast(F32),
                                                                            ALU.subtract), [th, aw_landed[n]])]
                    free["ex", 0] = made["aw", 2]

                t_neg = dve(lambda e: e.tensor_scalar(neg_id[:, :], ident[:, :], -1.0, None, ALU.mult))
                free, ready = {}, {}

                def front(b):
                    for i in range(NT):
                        t = dve(lambda e, i=i: e.bn_stats(raw[:, i, :], X[:, b, i, :]), x_ready[b])
                    for i in range(NT):
                        t = dve(lambda e, i=i: e.bn_aggr(mv[:, i, :], raw[:, i, :]), [t])
                    t = dve(lambda e: e.tensor_scalar(rs[:, 1, :], mv[:, :, 1], LN_EPS, None, ALU.add), [t])
                    yield
                    t = pool(lambda e: e.tensor_tensor(rs[:, 0, :], rs[:, 1, :], half_neg[:, 0:NT], ALU.pow), [t])
                    yield
                    for i in range(NT):
                        tx = dve(lambda e, i=i: e.tensor_scalar(xs[:, i, :], X[:, b, i, :], mv[:, i, 0:1], rs[:, 0, i:i + 1],
                                                                ALU.subtract, ALU.mult), [t, *free.get("xs", [])])
                    yield
                    hs = []
                    for k in range(KC):
                        tt, tp = transposed_split(xs, hT, 7, k, 1.0, [tx], free.get("hT", []))
                        hs += tt
                        free["xs"] = [tp]
                        yield

                    def queries_or_keys(slot):
                        w, dst, hg = (1, 0)[slot % 2], (ks, qs)[slot % 2][b % 2], slot // 2
                        terms = [(aw[w][:, y_, k, hg * P:(hg + 1) * P], hT[:, x_, k, :])
                                 for k in range(KC) for x_, y_ in ((0, 0), (1, 0), (0, 1))]
                        t = product(psum[:, 7, :], terms, [*made["aw", w], *hs, *bank_read[7]])
                        n = slot % 3
                        hi, lo, bc = parts[n][:, 0, :], parts[n][:, 1, :], abq[:, w, hg:hg + 1]
                        th = act(lambda e: e.activation(hi, psum[:, 7, :], ACT.Identity, bias=bc),
                                 [t, *made["abq"], *free.get(("part", n), [])])
                        tl = dve(lambda e: e.scalar_tensor_tensor(out=lo, in0=psum[:, 7, :], scalar=bc, in1=hi.bitcast(F32),
                                                                  op0=ALU.add, op1=ALU.subtract), [th])
                        bank_read[7] = [tl]
                        toks = []
                        for row, x_ in enumerate((0, 0, 1) if w == 0 else (0, 1, 0)):
                            for h in range(HQ):
                                tt = SP.do(lambda e, row=row, x_=x_, h=h: e.dma_start(
                                    dst[row * GD:(row + 1) * GD, hg * HQ + h, :].bitcast(F32),
                                    parts[n][h * GD:(h + 1) * GD, x_, :].bitcast(F32)),
                                    [th, tl, *free.get(("stack", b % 2), [])], s_st[slot * 3 + row])
                            toks.append(tt)
                        free["part", n] = toks
                        ready["stack", b, hg] = [*ready.get(("stack", b, hg), []), *toks]

                    def values_of(tiles):
                        n = len(tiles) * D
                        for c, i in enumerate(tiles):
                            t = product(psum[:, 7, c * D:(c + 1) * D], three(hT, i, aw[2]), [*made["aw", 2], *hs, *bank_read[7]], BV, D)
                        t = act(lambda e: e.activation(v[b % 2][:, tiles[0]:tiles[-1] + 1, :].rearrange("p i d -> p (i d)"),
                                                       psum[:, 7, 0:n], ACT.Copy), [t, *free.get(("v", b % 2), [])])
                        bank_read[7] = [t]
                        ready["v", b] = t

                    pieces = [(queries_or_keys, 0), (queries_or_keys, 1), (queries_or_keys, 2), (values_of, [0]),
                              (queries_or_keys, 3), (values_of, [1]), (values_of, [2, 3])]
                    if b == 0:
                        pieces.sort(key=lambda x: x[0] is values_of)
                    for piece, n in pieces:
                        piece(n)
                        yield
                    free["hT"] = [(s_pe, s_pe.count)]

                def of(u):
                    return u // (2 * NT), u // NT % 2, u % NT

                def half_banks(u, half):
                    return 2 * ((2 * u + half) % 3)

                def score(u, half):
                    b, nq, m = of(u)
                    b0 = half_banks(u, half)
                    for g in range(HH):
                        h = half * HH + g
                        dst = psum[:, b0 + g // 2, (g % 2) * NQ:(g % 2 + 1) * NQ]
                        t = pe(lambda e, h=h, dst=dst: e.matmul(dst, ks[b % 2][:, h, m * P:(m + 1) * P],
                                                                qs[b % 2][:, h, nq * NQ:(nq + 1) * NQ],
                                                                start=(h % 2 == 0), stop=False, skip_group_check=True),
                               [*ready["stack", b, half], *bank_read[b0], *bank_read[b0 + 1]])
                    ready["score", u, half] = t
                    if half and nq == 1 and m == NT - 1:
                        free["stack", b % 2] = [t]

                def heads(u, half):
                    b0 = half_banks(u, half)
                    return psum[:, b0:b0 + 2, :].rearrange("p k (g n) -> p (k g) n", g=2)

                def copy_first(u):
                    t = act(lambda e: e.activation(first[u % 2][:, :, :], heads(u, 0), ACT.Copy),
                            [ready["score", u, 0], *free.get(("first", u % 2), [])])
                    ready["first", u] = t

                def maximum(u):
                    t = dve(lambda e: e.tensor_tensor(tree[:, :, :], heads(u, 1), first[u % 2][:, :, :], ALU.max),
                            [ready["first", u], ready["score", u, 1], *free.get("tree", [])])
                    free["first", u % 2] = [t]
                    t = dve(lambda e: e.tensor_tensor(tree[:, 0:2, :], tree[:, 0:2, :], tree[:, 2:4, :], ALU.max), [t])
                    t = dve(lambda e: e.tensor_tensor(mr[u % 2][:, :], tree[:, 0, :], tree[:, 1, :], ALU.max),
                            [t, *free.get(("mr", u % 2), [])])
                    ready["max", u] = t
                    free["tree"] = [t]

                def shift(u, half):
                    b0 = half_banks(u, half)
                    for g in range(HH):
                        dst = psum[:, b0 + g // 2, (g % 2) * NQ:(g % 2 + 1) * NQ]
                        t = pe(lambda e, dst=dst: e.matmul(dst, neg_id[:, :], mr[u % 2][:, :], start=False, stop=True,
                                                           skip_group_check=True), [ready["max", u], t_neg])
                    te = act(lambda e: e.activation(ex[u % EXR][:, half * HH:(half + 1) * HH, :], heads(u, half), ACT.Exp,
                                                    scale=float(D) ** -0.5), [t, *free.get(("ex", u % EXR), [])])
                    bank_read[b0] = bank_read[b0 + 1] = [te]
                    free["mr", u % 2] = [t]
                    ready["ex", u] = [te]

                def total(u):
                    e_ = ex[u % EXR]
                    t = dve(lambda e: e.tensor_tensor(tree[:, :, :], e_[:, 0:4, :], e_[:, 4:8, :], ALU.add),
                            [*ready["ex", u], *free.get("tree", [])])
                    t = dve(lambda e: e.tensor_tensor(tree[:, 0:2, :], tree[:, 0:2, :], tree[:, 2:4, :], ALU.add), [t])
                    r = rec[u % 2]
                    t = dve(lambda e: e.tensor_tensor(r[:, :], tree[:, 0, :], tree[:, 1, :], ALU.add), [t, *free.get(("rec", u % 2), [])])
                    ready["total", u] = t
                    free["tree"] = [t]

                def inverse(u):
                    r = rec[u % 2]
                    t = act(lambda e: e.activation(r[:, :], r[:, :], ACT.Ln), [ready["total", u]])
                    t = act(lambda e: e.activation(r[:, :], r[:, :], ACT.Exp, scale=-1.0), [t])
                    ready["inverse", u] = t

                def normalise(u):
                    e_, r = ex[u % EXR], rec[u % 2]
                    by_total = r[:, :].unsqueeze(1).to_broadcast([P, G, NQ])
                    t = pool(lambda e: e.tensor_tensor(e_[:, :, :], e_[:, :, :], by_total, ALU.mult), [ready["inverse", u]])
                    free["rec", u % 2] = ready["probs", u] = [t]

                def values(u):
                    b, nq, m = of(u)
                    for hg in range(NHG):
                        for j in range(HQ):
                            h = hg * HQ + j
                            t = pe(lambda e, h=h, j=j, hg=hg: e.matmul(
                                psum[32 * j:32 * j + 32, 6, hg * NQ:(hg + 1) * NQ], v[b % 2][:, m, h * GD:(h + 1) * GD],
                                ex[u % EXR][:, h, :], start=(m == 0 and hg == 0), stop=(m == NT - 1), skip_group_check=True),
                                [ready["v", b], *ready["probs", u], *(bank_read[6] if m == 0 else ())])
                    free["ex", u % EXR] = [t]
                    if m < NT - 1:
                        return
                    if nq == 1:
                        free["v", b % 2] = [t]
                    tc = act(lambda e: e.activation(ct[:, :, :].rearrange("p g n -> p (g n)"), psum[:, 6, :], ACT.Copy),
                             [t, *free.get("ct", [])])
                    bank_read[6] = [tc]
                    ready["ct"] = tc

                def finish(u):
                    b, nq, m = of(u)
                    if m < NT - 1:
                        return
                    ni = NQ // P
                    for i in range(ni):
                        for hg in range(NHG):
                            t = pe(lambda e, i=i, hg=hg: e.transpose(psum[:, 7, (i * NHG + hg) * P:(i * NHG + hg + 1) * P],
                                                                     ct[:, hg, i * P:(i + 1) * P], ident[:, :]),
                                   [ready["ct"], *bank_read[7]])
                    free["ct"] = [t]
                    xv = X[:, b, nq * ni:(nq + 1) * ni, :].rearrange("p i d -> p (i d)")
                    t = dve(lambda e: e.tensor_tensor(xv, psum[:, 7, :], xv, ALU.add), [t])
                    bank_read[7] = [t]
                    x_ready[b] = [t]

                units = 2 * NT * B
                ahead = front(0)
                for _ in range(5):
                    next(ahead)
                split_weights()
                for _ in ahead:
                    pass
                ahead = front(1)
                score(0, 0)
                copy_first(0)
                for _ in range(4):
                    next(ahead)
                for u in range(units + 4):
                    b, it = u // (2 * NT), u % (2 * NT)
                    if it == 5:
                        later = front(b + 2) if b + 2 < B else iter(())
                    if 0 <= u - 1 < units:
                        shift(u - 1, 0)
                        shift(u - 1, 1)
                    if 0 <= u - 4 < units:
                        finish(u - 4)
                    if it in (4, 5, 6):
                        next(ahead, None)
                    if it == 6:
                        for _ in ahead:
                            pass
                        ahead = later
                        next(ahead, None)
                    if 0 <= u - 2 < units:
                        inverse(u - 2)
                    if u < units:
                        score(u, 1)
                        maximum(u)
                    if it in (0, 1, 2, 3, 4, 6, 7):
                        next(ahead, None)
                    if it == 5:
                        next(later, None)
                    if u + 1 < units:
                        score(u + 1, 0)
                        copy_first(u + 1)
                    if 0 <= u - 1 < units:
                        total(u - 1)
                    if 0 <= u - 2 < units:
                        normalise(u - 2)
                    if 0 <= u - 3 < units:
                        values(u - 3)
                with nc.Block() as block:
                    _issue(block, PE, DVE, SCA, POOL, SP)

        ffn("a")
        attention()
        ffn("b")


W_BACK, W_TOK, W_FRONT = 10, 22, 11
EXPAND = "VPVAVPAA"


def _issue(block, pe_lane, dve_lane, act_lane, pool_lane, sp_lane):
    @block.tensor
    def _(e):
        pe_lane.issue(e)

    @block.vector
    def _(e):
        dve_lane.issue(e)

    @block.scalar
    def _(e):
        act_lane.issue(e)

    @block.gpsimd
    def _(e):
        pool_lane.issue(e)

    @block.sync
    def _(e):
        sp_lane.issue(e)


_INS = ["L0_attn_hidden_states", "L0_attn_Wq", "L0_attn_bq", "L0_attn_Wk", "L0_attn_bk", "L0_attn_Wv", "L0_attn_bv",
        "L0_ffn_gamma1", "L0_ffn_Wq", "L0_ffn_bq", "L0_ffn_Wdown", "L0_ffn_bdown", "L0_ffn_Wup", "L0_ffn_bup",
        "L0_ffn_Wo", "L0_ffn_bo", "L0_ffn_gamma2", "L0_ffn_Wg", "L0_ffn_bg", "L0_ffn_We"]


def kernel(**inputs):
    import numpy as _np
    import concourse.bacc as _bacc
    from concourse.bass_utils import run_bass_kernel_spmd as _run

    nc = _bacc.Bacc("TRN2", target_bir_lowering=False, num_devices=1)
    arrays, aps = {}, {}
    for name in _INS:
        v = _np.ascontiguousarray(inputs[name])
        arrays[f"in_{name}"] = v
        aps[name] = nc.dram_tensor(f"in_{name}", v.shape, mybir.dt.from_np(v.dtype), kind="ExternalInput").ap()
    shape = arrays["in_L0_attn_hidden_states"].shape
    out = nc.dram_tensor("out", shape, F32, kind="ExternalOutput").ap()
    macaron(nc, aps, out)
    r = _run(nc, [arrays], core_ids=[0])
    return r.results[0]["out"]
```
